# Optimizing a Trainium2 kernel written in Bass

```python
import numpy as np
import jax
import jax.numpy as jnp

def _softmax(x, axis=-1):
    return jax.nn.softmax(x, axis=axis)

def _gelu(x):
    return jax.nn.gelu(x, approximate=True)

def _silu(x):
    return jax.nn.silu(x)

def _sigmoid(x):
    return jax.nn.sigmoid(x)

def _layernorm(x, axis=-1, eps=1e-05):
    m = jnp.mean(x, axis=axis, keepdims=True)
    v = jnp.var(x, axis=axis, keepdims=True)
    return (x - m) / jnp.sqrt(v + eps)

def _scatter_add(tgt, idx, src, axis=0):
    return tgt.at[idx].add(src)

def _segment_sum(src, seg, n):
    return jax.ops.segment_sum(src, seg, n)
kernel_name = 'mk_dlrm_tower_d1_rec_r8_109305'

def setup_inputs(seed: int=0):
    np.random.seed(seed)
    _w = jnp.asarray

    def _rec_inputs():
        import jax
        import jax.numpy as jnp
        _tk = jax.random.key(seed)
        ids = jnp.stack([jax.random.randint(jax.random.fold_in(_tk, 200 + f), (2048,), 0, v, jnp.int32) for f, v in enumerate([1250, 1250, 12500, 12500, 12500, 12500, 1250, 1250, 1000, 1000, 1000, 125000, 1250, 1000, 1250, 1250, 12500, 12500, 1250, 1000, 12500, 1000, 12500, 1250, 1250, 1250])], axis=1)
        tbl_0 = 0.05 * jax.random.normal(jax.random.fold_in(_tk, 500 + 0), (1250, 128), jnp.float32)
        tbl_1 = 0.05 * jax.random.normal(jax.random.fold_in(_tk, 500 + 1), (1250, 128), jnp.float32)
        tbl_2 = 0.05 * jax.random.normal(jax.random.fold_in(_tk, 500 + 2), (12500, 128), jnp.float32)
        tbl_3 = 0.05 * jax.random.normal(jax.random.fold_in(_tk, 500 + 3), (12500, 128), jnp.float32)
        tbl_4 = 0.05 * jax.random.normal(jax.random.fold_in(_tk, 500 + 4), (12500, 128), jnp.float32)
        tbl_5 = 0.05 * jax.random.normal(jax.random.fold_in(_tk, 500 + 5), (12500, 128), jnp.float32)
        tbl_6 = 0.05 * jax.random.normal(jax.random.fold_in(_tk, 500 + 6), (1250, 128), jnp.float32)
        tbl_7 = 0.05 * jax.random.normal(jax.random.fold_in(_tk, 500 + 7), (1250, 128), jnp.float32)
        tbl_8 = 0.05 * jax.random.normal(jax.random.fold_in(_tk, 500 + 8), (1000, 128), jnp.float32)
        tbl_9 = 0.05 * jax.random.normal(jax.random.fold_in(_tk, 500 + 9), (1000, 128), jnp.float32)
        tbl_10 = 0.05 * jax.random.normal(jax.random.fold_in(_tk, 500 + 10), (1000, 128), jnp.float32)
        tbl_11 = 0.05 * jax.random.normal(jax.random.fold_in(_tk, 500 + 11), (125000, 128), jnp.float32)
        tbl_12 = 0.05 * jax.random.normal(jax.random.fold_in(_tk, 500 + 12), (1250, 128), jnp.float32)
        tbl_13 = 0.05 * jax.random.normal(jax.random.fold_in(_tk, 500 + 13), (1000, 128), jnp.float32)
        tbl_14 = 0.05 * jax.random.normal(jax.random.fold_in(_tk, 500 + 14), (1250, 128), jnp.float32)
        tbl_15 = 0.05 * jax.random.normal(jax.random.fold_in(_tk, 500 + 15), (1250, 128), jnp.float32)
        tbl_16 = 0.05 * jax.random.normal(jax.random.fold_in(_tk, 500 + 16), (12500, 128), jnp.float32)
        tbl_17 = 0.05 * jax.random.normal(jax.random.fold_in(_tk, 500 + 17), (12500, 128), jnp.float32)
        tbl_18 = 0.05 * jax.random.normal(jax.random.fold_in(_tk, 500 + 18), (1250, 128), jnp.float32)
        tbl_19 = 0.05 * jax.random.normal(jax.random.fold_in(_tk, 500 + 19), (1000, 128), jnp.float32)
        tbl_20 = 0.05 * jax.random.normal(jax.random.fold_in(_tk, 500 + 20), (12500, 128), jnp.float32)
        tbl_21 = 0.05 * jax.random.normal(jax.random.fold_in(_tk, 500 + 21), (1000, 128), jnp.float32)
        tbl_22 = 0.05 * jax.random.normal(jax.random.fold_in(_tk, 500 + 22), (12500, 128), jnp.float32)
        tbl_23 = 0.05 * jax.random.normal(jax.random.fold_in(_tk, 500 + 23), (1250, 128), jnp.float32)
        tbl_24 = 0.05 * jax.random.normal(jax.random.fold_in(_tk, 500 + 24), (1250, 128), jnp.float32)
        tbl_25 = 0.05 * jax.random.normal(jax.random.fold_in(_tk, 500 + 25), (1250, 128), jnp.float32)
        _rk = jax.random.fold_in(_tk, 7)
        r_dense_features = -0.000520686 + 1.00062 * jax.random.normal(jax.random.fold_in(_rk, 101), (2048, 128), jnp.float32)
        W_top1 = 0.0405887 * jax.random.normal(jax.random.fold_in(_tk, 801), (607, 512), jnp.float32)
        W_top2 = 0.0441942 * jax.random.normal(jax.random.fold_in(_tk, 802), (512, 256), jnp.float32)
        W_top3 = 0.0625 * jax.random.normal(jax.random.fold_in(_tk, 803), (256, 1), jnp.float32)
        b_top1 = jnp.zeros((512,), jnp.float32)
        b_top2 = jnp.zeros((256,), jnp.float32)
        return (r_dense_features, ids, tbl_0, tbl_1, tbl_2, tbl_3, tbl_4, tbl_5, tbl_6, tbl_7, tbl_8, tbl_9, tbl_10, tbl_11, tbl_12, tbl_13, tbl_14, tbl_15, tbl_16, tbl_17, tbl_18, tbl_19, tbl_20, tbl_21, tbl_22, tbl_23, tbl_24, tbl_25, W_top1, b_top1, W_top2, b_top2, W_top3)
    r_dense_features, ids, tbl_0, tbl_1, tbl_2, tbl_3, tbl_4, tbl_5, tbl_6, tbl_7, tbl_8, tbl_9, tbl_10, tbl_11, tbl_12, tbl_13, tbl_14, tbl_15, tbl_16, tbl_17, tbl_18, tbl_19, tbl_20, tbl_21, tbl_22, tbl_23, tbl_24, tbl_25, W_top1, b_top1, W_top2, b_top2, W_top3 = _rec_inputs()

    def _L0_rec_setup():
        import jax, jax.numpy as jnp
        import numpy as np
        F = 26
        B, D = (2048, 128)
        _IU0, _IU1 = np.triu_indices(F + 1, k=1)
        _IU0 = jnp.asarray(_IU0)
        _IU1 = jnp.asarray(_IU1)
        key = jax.random.key(seed)
        k1, k2 = jax.random.split(key)
        dense_features = jax.random.normal(k1, (B, D), dtype=jnp.float32)
        sparse_features = jax.random.normal(k2, (B, F, D), dtype=jnp.float32)
        return {'dense_features': dense_features, 'sparse_features': sparse_features}
    _L0_rec_all = _L0_rec_setup()
    _L0_rec_in = {k: v for k, v in _L0_rec_all.items() if k in ()}
    del _L0_rec_all
    return {'r_dense_features': r_dense_features, 'ids': ids, 'tbl_0': tbl_0, 'tbl_1': tbl_1, 'tbl_2': tbl_2, 'tbl_3': tbl_3, 'tbl_4': tbl_4, 'tbl_5': tbl_5, 'tbl_6': tbl_6, 'tbl_7': tbl_7, 'tbl_8': tbl_8, 'tbl_9': tbl_9, 'tbl_10': tbl_10, 'tbl_11': tbl_11, 'tbl_12': tbl_12, 'tbl_13': tbl_13, 'tbl_14': tbl_14, 'tbl_15': tbl_15, 'tbl_16': tbl_16, 'tbl_17': tbl_17, 'tbl_18': tbl_18, 'tbl_19': tbl_19, 'tbl_20': tbl_20, 'tbl_21': tbl_21, 'tbl_22': tbl_22, 'tbl_23': tbl_23, 'tbl_24': tbl_24, 'tbl_25': tbl_25, 'W_top1': W_top1, 'b_top1': b_top1, 'W_top2': W_top2, 'b_top2': b_top2, 'W_top3': W_top3}

def reference(r_dense_features, ids, tbl_0, tbl_1, tbl_2, tbl_3, tbl_4, tbl_5, tbl_6, tbl_7, tbl_8, tbl_9, tbl_10, tbl_11, tbl_12, tbl_13, tbl_14, tbl_15, tbl_16, tbl_17, tbl_18, tbl_19, tbl_20, tbl_21, tbl_22, tbl_23, tbl_24, tbl_25, W_top1, b_top1, W_top2, b_top2, W_top3):
    import jax
    import jax.numpy as jnp

    def _L0_rec_ref(dense_features, sparse_features):
        import jax, jax.numpy as jnp
        import numpy as np
        F = 26
        B, D = (2048, 128)
        _IU0, _IU1 = np.triu_indices(F + 1, k=1)
        _IU0 = jnp.asarray(_IU0)
        _IU1 = jnp.asarray(_IU1)
        combined = jnp.concatenate([dense_features[:, None, :], sparse_features], axis=1)
        interactions = jnp.einsum('bfd,bgd->bfg', combined, combined)
        interactions_flat = interactions[:, _IU0, _IU1]
        return jnp.concatenate([dense_features, interactions_flat], axis=1)
    e = jnp.stack([tbl_0[ids[:, 0]], tbl_1[ids[:, 1]], tbl_2[ids[:, 2]], tbl_3[ids[:, 3]], tbl_4[ids[:, 4]], tbl_5[ids[:, 5]], tbl_6[ids[:, 6]], tbl_7[ids[:, 7]], tbl_8[ids[:, 8]], tbl_9[ids[:, 9]], tbl_10[ids[:, 10]], tbl_11[ids[:, 11]], tbl_12[ids[:, 12]], tbl_13[ids[:, 13]], tbl_14[ids[:, 14]], tbl_15[ids[:, 15]], tbl_16[ids[:, 16]], tbl_17[ids[:, 17]], tbl_18[ids[:, 18]], tbl_19[ids[:, 19]], tbl_20[ids[:, 20]], tbl_21[ids[:, 21]], tbl_22[ids[:, 22]], tbl_23[ids[:, 23]], tbl_24[ids[:, 24]], tbl_25[ids[:, 25]]], axis=1)
    z = _L0_rec_ref(r_dense_features, e)
    z = z.reshape(z.shape[0], -1)
    h = jnp.concatenate([z, r_dense_features], axis=1)
    h = jnp.maximum(h @ W_top1 + b_top1, 0.0)
    h = jnp.maximum(h @ W_top2 + b_top2, 0.0)
    y = h @ W_top3
    return y

_drawn_inputs = setup_inputs


def setup_inputs(seed=0):
    import zlib

    import numpy as np

    out = dict(_drawn_inputs(seed))
    spreads = {'b_top1': (0.0, 0.1), 'b_top2': (0.0, 0.1)}
    factors = {}
    for name, (base, spread) in spreads.items():
        noise = np.random.default_rng([zlib.crc32(name.encode()), seed]).standard_normal(out[name].shape)
        drawn = base * np.exp(spread * noise) if base else spread * noise
        out[name] = jnp.asarray(drawn.astype(out[name].dtype))
    for name, factor in factors.items():
        out[name] = (out[name] * factor).astype(out[name].dtype)
    return out
```

```python
import numpy as np
import concourse.bass as bass
from concourse import mybir
from contextlib import ExitStack

F32 = mybir.dt.float32
I32 = mybir.dt.int32
ACT = mybir.ActivationFunctionType
ALU = mybir.AluOpType

BATCH, DIM, TABLES = 2048, 128, 26
FEATURES = TABLES + 1
HID1, HID2 = 512, 256
PAIRS = FEATURES * (FEATURES - 1) // 2

P = 128
TILE, TILES_PER_CHUNK = P, 4
CHUNK = TILE * TILES_PER_CHUNK
CHUNKS = BATCH // CHUNK
MEMBERS, GROUPS = 4, TILE // 4
SLOT = P // MEMBERS
CHUNK_GROUPS = GROUPS * TILES_PER_CHUNK
GROUP_COLS = MEMBERS * FEATURES
BATCH_GROUPS = 4
GRAM_BATCHES = GROUPS // BATCH_GROUPS

GATHERED = list(range(TABLES))
PLACE_OF_TABLE = {f: 1 + n for n, f in enumerate(GATHERED)}
UNIT = 4
UNITS = [GATHERED[n:n + UNIT] for n in range(0, len(GATHERED), UNIT)]
UNITS_PER_CHUNK = TILES_PER_CHUNK * len(UNITS)

SHIFTS = (FEATURES - 1) // 2
PAIR_TILES = 3
PAIR_F = FEATURES // PAIR_TILES
PAIR_ROWS = SHIFTS * PAIR_F
WRAP_F = FEATURES - SHIFTS

H1_TILES, H2_TILES = HID1 // P, HID2 // P
ACCS = H1_TILES + H2_TILES + 1
MLP_ITEMS = ([(m, k) for m in range(H1_TILES) for k in range(PAIR_TILES + 1)]
             + [(H1_TILES + m, k) for m in range(H2_TILES) for k in range(H1_TILES)]
             + [(ACCS - 1, k) for k in range(H2_TILES)])
MLP_STEPS = [(j, u) for j in range(1, TILES_PER_CHUNK) for u in range(len(UNITS)) if j > 1 or u > 3]


def share(items, steps, n):
    return items[len(items) * n // steps:len(items) * (n + 1) // steps]


def gram_share(u):
    return share(list(range(GRAM_BATCHES)), len(UNITS), u)


def mlp_share(j, u):
    return share(MLP_ITEMS, len(MLP_STEPS), MLP_STEPS.index((j, u))) if (j, u) in MLP_STEPS else []


def build(nc, ids, x_t, tables, w_pairs, w_dense_a, w_dense_b, b1, w2, b2, w3, eye, out):
    ids_t = ids.rearrange("(t p) f -> t p f", p=P)
    x_tiles = x_t.rearrange("d (t p) -> t d p", p=TILE)
    x_chunks = x_t.rearrange("d (c n) -> c d n", n=CHUNK)
    out_v = out.rearrange("(c j s q) o -> c o s j q", j=TILES_PER_CHUNK, s=MEMBERS, q=GROUPS)
    scratch = nc.dram_tensor("gram_scratch", [FEATURES + SHIFTS, MEMBERS, FEATURES, CHUNK_GROUPS], F32)
    scratch_ap = scratch.ap()

    with ExitStack() as ctx:
        def sb(name, shape, dt=F32):
            return ctx.enter_context(nc.sbuf_tensor(name, shape, dt))

        def pb(name):
            return ctx.enter_context(nc.psum_tensor(name, [P, 512], F32))

        def sem(name):
            return ctx.enter_context(nc.semaphore(name))

        index = sb("index", [P, 2, TABLES], I32)
        rows = sb("rows", [P, 2, len(GATHERED), DIM])
        x_tile = sb("x_tile", [P, 2, TILE])
        emb = sb("emb", [P, TILES_PER_CHUNK, GROUPS, MEMBERS, SLOT])
        gram = sb("gram", [P, 2, FEATURES, CHUNK_GROUPS])
        pairs = sb("pairs", [PAIR_ROWS, PAIR_TILES, MEMBERS, CHUNK_GROUPS])
        x_mlp = sb("x_mlp", [P, CHUNK])
        wp_sb = sb("wp_sb", [PAIR_ROWS, PAIR_TILES, HID1])
        wx_sb = sb("wx_sb", [P, HID1])
        wxb_sb = sb("wxb_sb", [P, HID1])
        w2_sb = sb("w2_sb", [P, H1_TILES, HID2])
        w3_sb = sb("w3_sb", [P, H2_TILES])
        b1_sb = sb("b1_sb", [P, H1_TILES])
        b2_sb = sb("b2_sb", [P, H2_TILES])
        eye_sb = sb("eye_sb", [P, P])
        h1 = sb("h1", [P, H1_TILES, CHUNK])
        h2 = sb("h2", [P, H2_TILES, CHUNK])
        y_row = sb("y_row", [1, CHUNK])

        unit_ps = [pb(f"unit_ps{i}") for i in range(2)]
        gram_ps = [pb(f"gram_ps{i}") for i in range(2)]
        mlp_ps = [pb(f"mlp_ps{i}") for i in range(2)]

        index_in = [sem(f"index_in{i}") for i in range(2)]
        x_in = [sem(f"x_in{i}") for i in range(2)]
        gathered = [[sem(f"gathered{i}_{u}") for u in range(len(UNITS))] for i in range(2)]
        weights_in = sem("weights_in")
        eye_in = sem("eye_in")
        dense_summed = sem("dense_summed")
        spare_zeroed = sem("spare_zeroed")
        x_placed = sem("x_placed")
        unit_ready, unit_taken = sem("unit_ready"), sem("unit_taken")
        gram_ready, gram_taken = sem("gram_ready"), sem("gram_taken")
        scratch_out, mlp_in = sem("scratch_out"), sem("mlp_in")
        mlp_ready = sem("mlp_ready")
        h1_taken, h2_taken, y_taken = sem("h1_taken"), sem("h2_taken"), sem("y_taken")
        y_out = sem("y_out")
        gram_left = sem("gram_left")
        units_opened, loads_opened = sem("units_opened"), sem("loads_opened")

        WEIGHT_DMAS, SCRATCH_DMAS, MLP_DMAS = 7, 2 * MEMBERS, MEMBERS * PAIR_TILES + 1

        def emb_place(j, place, n):
            return emb[:, j, :, :, place:place + n].rearrange("d q s f -> d f s q")

        def unit_index(j, u):
            return j * len(UNITS) + u

        block = ctx.enter_context(nc.Block())

        @block.sync
        def _(sp):
            def load_tile(c, j):
                i = j % 2
                if not (isinstance(c, int) and c == 0 and j < 2):
                    back = unit_index(j - 2, len(UNITS) - 1) if j >= 2 else \
                        unit_index(j + 2, len(UNITS) - 1) - UNITS_PER_CHUNK
                    sp.wait_ge(unit_ready, UNITS_PER_CHUNK * c + back + 1)
                    sp.sem_inc(loads_opened, 1)
                sp.dma_start(index[:, i, :], ids_t[c * TILES_PER_CHUNK + j]).then_inc(index_in[i], 16)
                if not (isinstance(c, int) and c == 0 and j < 2):
                    sp.wait_ge(x_placed, TILES_PER_CHUNK * c + j - 1)
                    sp.sem_inc(loads_opened, 1)
                sp.dma_start(x_tile[:, i, :], x_tiles[c * TILES_PER_CHUNK + j]).then_inc(x_in[i], 16)

            def bounce(c):
                sp.wait_ge(gram_taken, GRAM_BATCHES * TILES_PER_CHUNK * (c + 1))
                sp.sem_inc(loads_opened, 1)
                half = c % 2
                for s in range(MEMBERS):
                    r = SLOT * s
                    sp.dma_start(scratch_ap[0:FEATURES, s, :, :],
                                 gram[r:r + FEATURES, half]).then_inc(scratch_out, 16)
                    sp.dma_start(scratch_ap[FEATURES:FEATURES + SHIFTS, s, WRAP_F:, :],
                                 gram[r:r + SHIFTS, half, WRAP_F:, :]).then_inc(scratch_out, 16)
                sp.wait_ge(scratch_out, 16 * SCRATCH_DMAS * (c + 1))
                sp.sem_inc(gram_left, 1)
                sp.wait_ge(h1_taken, H1_TILES * c + 1)
                sp.sem_inc(loads_opened, 1)
                row = MEMBERS * FEATURES * CHUNK_GROUPS
                for s in range(MEMBERS):
                    for k in range(PAIR_TILES):
                        first = scratch_ap[1 + PAIR_F * k, s, PAIR_F * k, :]
                        src = bass.AP(tensor=first.tensor, offset=first.offset,
                                      ap=[[row, SHIFTS], [row + CHUNK_GROUPS, PAIR_F], [1, CHUNK_GROUPS]])
                        sp.dma_start(pairs[:, k, s], src).then_inc(mlp_in, 16)
                sp.dma_start(x_mlp[:, :], x_chunks[c]).then_inc(mlp_in, 16)
                sp.wait_ge(mlp_in, 16 * MLP_DMAS * (c + 1))
                sp.sem_inc(loads_opened, 1)

            sp.sem_inc(gram_left, 1)
            load_tile(0, 0)
            sp.dma_start(eye_sb[:, :], eye).then_inc(eye_in, 16)
            for j in range(1, TILES_PER_CHUNK):
                load_tile(0, j)
            with sp.Fori(1, CHUNKS) as c:
                for j in range(3):
                    load_tile(c, j)
                bounce(c - 1)
                load_tile(c, 3)
            bounce(CHUNKS - 1)

        @block.gpsimd
        def _(pool):
            def gather_tile(c, j):
                i, lap = j % 2, 2 * c + j // 2
                pool.wait_ge(index_in[i], 16 * (lap + 1))
                pool.sem_inc(units_opened, 1)
                for u, unit in enumerate(UNITS):
                    if not (isinstance(c, int) and c == 0 and j < 2):
                        back = unit_index(j - 2, u) if j >= 2 else unit_index(j + 2, u) - UNITS_PER_CHUNK
                        pool.wait_ge(unit_ready, UNITS_PER_CHUNK * c + back + 1)
                        pool.sem_inc(units_opened, 1)
                    for f in unit:
                        n = PLACE_OF_TABLE[f] - 1
                        nc.gpsimd.indirect_dma_start(
                            out=rows[:, i, n, :], out_offset=None, in_=tables[f],
                            in_offset=bass.IndirectOffsetOnAxis(ap=index[:, i, f:f + 1], axis=0),
                        ).then_inc(gathered[i][u], 16)

            for j in range(TILES_PER_CHUNK):
                gather_tile(0, j)
            with pool.Fori(1, CHUNKS) as c:
                for j in range(TILES_PER_CHUNK):
                    gather_tile(c, j)

        def mlp_operands(acc, k):
            if acc < H1_TILES:
                m = slice(acc * P, (acc + 1) * P)
                if k < PAIR_TILES:
                    return wp_sb[:, k, m], pairs[:, k, :, :]
                return wx_sb[:, m], x_mlp[:, :].rearrange("d (j s q) -> d s j q", j=TILES_PER_CHUNK, s=MEMBERS)
            if acc < H1_TILES + H2_TILES:
                m = acc - H1_TILES
                return w2_sb[:, k, m * P:(m + 1) * P], h1[:, k, :]
            return w3_sb[:, k:k + 1], h2[:, k, :]

        @block.tensor
        def _(pe):
            def unit(c, j, u):
                n, i, lap = unit_index(j, u), j % 2, 2 * c + j // 2
                pe.wait_ge(gathered[i][u], 16 * len(UNITS[u]) * (lap + 1))
                if not (isinstance(c, int) and c == 0 and n < 2):
                    pe.wait_ge(unit_taken, UNITS_PER_CHUNK * c + n - 1)
                for a, f in enumerate(UNITS[u]):
                    last = nc.tensor.transpose(unit_ps[n % 2][:, a * TILE:(a + 1) * TILE],
                                               rows[:, i, PLACE_OF_TABLE[f] - 1, :], eye_sb[:, :])
                last.then_inc(unit_ready, 1)

            def gram_batch(c, j, b):
                if b == 0:
                    pe.wait_ge(unit_taken, UNITS_PER_CHUNK * c + unit_index(j, len(UNITS) - 1) + 1)
                    pe.wait_ge(x_placed, TILES_PER_CHUNK * c + j + 1)
                n = GRAM_BATCHES * j + b
                if not (isinstance(c, int) and c == 0 and n < 2):
                    pe.wait_ge(gram_taken, GRAM_BATCHES * TILES_PER_CHUNK * c + n - 1)
                for a in range(BATCH_GROUPS):
                    q = b * BATCH_GROUPS + a
                    last = nc.tensor.matmul(gram_ps[b % 2][:, a * GROUP_COLS:(a + 1) * GROUP_COLS],
                                            emb[:, j, q, :, :].rearrange("d s f -> d (s f)"), emb[:, j, q, :, 0:FEATURES], start=True, stop=True)
                last.then_inc(gram_ready, 1)

            def mlp_item(c, acc, k):
                if acc == 0 and k == 0:
                    pe.wait_ge(mlp_in, 16 * MLP_DMAS * (c + 1))
                    pe.wait_ge(y_taken, c + 1)
                if acc == 1 and k == 0:
                    pe.wait_ge(h2_taken, H2_TILES * c + 1)
                if 2 <= acc < H1_TILES and k == 0:
                    pe.wait_ge(h1_taken, H1_TILES * c + acc)
                if acc == H1_TILES and k == 0:
                    pe.wait_ge(h1_taken, H1_TILES * (c + 1) + 1)
                if acc == ACCS - 1 and k == 0:
                    pe.wait_ge(h2_taken, H2_TILES * (c + 1) + 1)
                last_k = {True: PAIR_TILES, False: H1_TILES - 1}[acc < H1_TILES] if acc < ACCS - 1 else H2_TILES - 1
                lhs, rhs = mlp_operands(acc, k)
                o = mlp_ps[acc % 2][0:1, :] if acc == ACCS - 1 else mlp_ps[acc % 2][:, :]
                mm = nc.tensor.matmul(o, lhs, rhs, start=(k == 0), stop=(k == last_k))
                if k == last_k:
                    mm.then_inc(mlp_ready, 1)

            def chunk(c, first):
                for j in range(TILES_PER_CHUNK):
                    for u in range(len(UNITS)):
                        unit(c, j, u)
                        if j > 0 or not first:
                            for b in gram_share(u):
                                gram_batch(c if j else c - 1, (j - 1) % TILES_PER_CHUNK, b)
                        if not first:
                            for acc, k in mlp_share(j, u):
                                mlp_item(c - 1, acc, k)

            pe.wait_ge(eye_in, 16)
            pe.wait_ge(spare_zeroed, 1)
            chunk(0, True)
            pe.wait_ge(weights_in, 16 * WEIGHT_DMAS)
            pe.wait_ge(dense_summed, 1)
            with pe.Fori(1, CHUNKS) as c:
                chunk(c, False)
            for b in range(GRAM_BATCHES):
                gram_batch(CHUNKS - 1, TILES_PER_CHUNK - 1, b)
            for acc, k in MLP_ITEMS:
                mlp_item(CHUNKS - 1, acc, k)

        @block.scalar
        def _(act):
            for started, n in ((h1_taken, 1), (h2_taken, 1), (y_taken, 1), (y_out, 16)):
                act.sem_inc(started, n)
            for dst, src in ((wp_sb, w_pairs), (wx_sb, w_dense_a), (wxb_sb, w_dense_b), (w2_sb, w2),
                             (w3_sb, w3), (b1_sb, b1), (b2_sb, b2)):
                act.dma_start(dst[:], src).then_inc(weights_in, 16)

            def slot_free(c, j):
                if not (isinstance(c, int) and c == 0):
                    act.wait_ge(gram_ready, GRAM_BATCHES * TILES_PER_CHUNK * c
                                + GRAM_BATCHES * (j + 1 - TILES_PER_CHUNK))

            def place_x(c, j):
                act.wait_ge(x_in[j % 2], 16 * (2 * c + j // 2 + 1))
                nc.scalar.copy(emb_place(j, 0, 1)[:, 0],
                               x_tile[:, j % 2, :].rearrange("d (s q) -> d s q", s=MEMBERS)).then_inc(x_placed, 1)

            def take_unit(c, j, u):
                n = unit_index(j, u)
                act.wait_ge(unit_ready, UNITS_PER_CHUNK * c + n + 1)
                k = len(UNITS[u])
                src = unit_ps[n % 2][:, 0:k * TILE].rearrange("d (f s q) -> d f s q", f=k, s=MEMBERS)
                nc.scalar.copy(emb_place(j, PLACE_OF_TABLE[UNITS[u][0]], k), src).then_inc(unit_taken, 1)

            def take_acc(c, acc):
                act.wait_ge(mlp_ready, ACCS * c + acc + 1)
                if acc < H1_TILES:
                    nc.scalar.activation(h1[:, acc, :], mlp_ps[acc % 2][:, :], ACT.Relu,
                                         bias=b1_sb[:, acc:acc + 1]).then_inc(h1_taken, 1)
                elif acc < ACCS - 1:
                    m = acc - H1_TILES
                    nc.scalar.activation(h2[:, m, :], mlp_ps[acc % 2][:, :], ACT.Relu,
                                         bias=b2_sb[:, m:m + 1]).then_inc(h2_taken, 1)
                else:
                    act.wait_ge(y_out, 16 * (c + 1))
                    nc.scalar.copy(y_row[:, :], mlp_ps[acc % 2][0:1, :]).then_inc(y_taken, 1)
                    act.wait_ge(y_taken, c + 2)
                    act.dma_start(out_v[c], y_row[:, :].rearrange("o (s j q) -> o s j q", s=MEMBERS,
                                                                  j=TILES_PER_CHUNK)).then_inc(y_out, 16)

            def accs_ended(items):
                last = {acc: k for acc, k in MLP_ITEMS}
                return [acc for acc, k in items if last[acc] == k]

            def chunk(c, first):
                for j in range(TILES_PER_CHUNK):
                    slot_free(c, j)
                    place_x(c, j)
                    for u in range(len(UNITS)):
                        take_unit(c, j, u)
                        if not first:
                            for acc in accs_ended(mlp_share(j, u)):
                                take_acc(c - 1, acc)

            chunk(0, True)
            act.wait_ge(weights_in, 16 * WEIGHT_DMAS)
            with act.Fori(1, CHUNKS) as c:
                chunk(c, False)
            for acc in range(ACCS):
                take_acc(CHUNKS - 1, acc)
            act.wait_ge(y_out, 16 * (CHUNKS + 1))

        @block.vector
        def _(dve):
            nc.vector.memset(emb[:, :, :, :, FEATURES:SLOT].rearrange("d j q s f -> d (j q s) f"),
                             0.0).then_inc(spare_zeroed, 1)
            dve.wait_ge(weights_in, 16 * WEIGHT_DMAS)
            nc.vector.tensor_tensor(wx_sb[:, :], wx_sb[:, :], wxb_sb[:, :], ALU.add).then_inc(dense_summed, 1)

            def take_batch(c, j, b):
                dve.wait_ge(gram_ready, GRAM_BATCHES * TILES_PER_CHUNK * c + GRAM_BATCHES * j + b + 1)
                g0 = j * GROUPS + b * BATCH_GROUPS
                for s in range(MEMBERS):
                    r = slice(SLOT * s, SLOT * (s + 1))
                    src = gram_ps[b % 2][r, 0:BATCH_GROUPS * GROUP_COLS].rearrange(
                        "g (q n) -> g q n", q=BATCH_GROUPS)[:, :, s * FEATURES:(s + 1) * FEATURES]
                    dst = gram[r, c % 2, :, g0:g0 + BATCH_GROUPS].rearrange("g f q -> g q f")
                    last = nc.vector.tensor_copy(dst, src)
                last.then_inc(gram_taken, 1)

            def chunk(c, first):
                for j in range(TILES_PER_CHUNK):
                    if j == 1 and not first:
                        dve.wait_ge(gram_left, c)
                    if j > 0 or not first:
                        for b in range(GRAM_BATCHES):
                            take_batch(c if j else c - 1, (j - 1) % TILES_PER_CHUNK, b)

            chunk(0, True)
            with dve.Fori(1, CHUNKS) as c:
                chunk(c, False)
            for b in range(GRAM_BATCHES):
                take_batch(CHUNKS - 1, TILES_PER_CHUNK - 1, b)


def pair_rows():
    table_at = [0] + [1 + f for f in GATHERED]
    index = {}
    for i in range(FEATURES):
        for j in range(i + 1, FEATURES):
            index[i, j] = len(index)
    found = np.zeros((PAIR_ROWS, PAIR_TILES), np.int64)
    for k in range(PAIR_TILES):
        for d in range(SHIFTS):
            for n in range(PAIR_F):
                f = PAIR_F * k + n
                a, b = table_at[f], table_at[(f + d + 1) % FEATURES]
                found[d * PAIR_F + n, k] = index[min(a, b), max(a, b)]
    return found


def kernel(**inputs):
    import concourse.bacc as bacc
    from concourse.bass_utils import run_bass_kernel_spmd

    a = {k: np.ascontiguousarray(v) for k, v in inputs.items()}
    w1 = a["W_top1"]
    arrays = {
        "ids": a["ids"],
        "x_t": np.ascontiguousarray(a["r_dense_features"].T),
        "w_pairs": np.ascontiguousarray(w1[DIM:DIM + PAIRS][pair_rows()]),
        "w_dense_a": np.ascontiguousarray(w1[:DIM]),
        "w_dense_b": np.ascontiguousarray(w1[DIM + PAIRS:]),
        "b1": np.ascontiguousarray(a["b_top1"].reshape(H1_TILES, P).T),
        "w2": np.ascontiguousarray(a["W_top2"].reshape(H1_TILES, P, HID2).transpose(1, 0, 2)),
        "b2": np.ascontiguousarray(a["b_top2"].reshape(H2_TILES, P).T),
        "w3": np.ascontiguousarray(a["W_top3"].reshape(H2_TILES, P).T),
        "eye": np.eye(P, dtype=np.float32),
    }
    for f in range(TABLES):
        arrays[f"tbl_{f}"] = a[f"tbl_{f}"]
    nc = bacc.Bacc("TRN2", target_bir_lowering=False, num_devices=1)
    ap = {k: nc.dram_tensor(k, v.shape, mybir.dt.from_np(v.dtype), kind="ExternalInput").ap()
          for k, v in arrays.items()}
    out = nc.dram_tensor("y", (BATCH, 1), F32, kind="ExternalOutput").ap()
    build(nc, ap["ids"], ap["x_t"], [ap[f"tbl_{f}"] for f in range(TABLES)], ap["w_pairs"], ap["w_dense_a"],
          ap["w_dense_b"], ap["b1"], ap["w2"], ap["b2"], ap["w3"], ap["eye"], out)
    r = run_bass_kernel_spmd(nc, [arrays], core_ids=[0])
    return r.results[0]["y"]
```

```python
import numpy as np
import concourse.bass as bass
from concourse import mybir
from contextlib import ExitStack

F32 = mybir.dt.float32
F32R = mybir.dt.float32r
I32 = mybir.dt.int32
ACT = mybir.ActivationFunctionType
ALU = mybir.AluOpType

BATCH, DIM, TABLES = 2048, 128, 26
FEATURES = TABLES + 1
HID1, HID2 = 512, 256
PAIRS = FEATURES * (FEATURES - 1) // 2

P = 128
TILE, CHUNK_TILES, LAP_TILES = P, 2, 4
TILES = BATCH // TILE
CHUNK = TILE * CHUNK_TILES
CHUNKS = BATCH // CHUNK
LAPS = TILES // LAP_TILES
MEMBERS, GROUPS = 4, TILE // 4
CHUNK_GROUPS = GROUPS * CHUNK_TILES
GROUP_COLS = MEMBERS * FEATURES
BATCH_GROUPS = 4
GRAM_BATCHES = GROUPS // BATCH_GROUPS

PICKED = [8, 9, 10, 13, 19, 21]
PICKED_ROWS = 1000
GATHERED = [f for f in range(TABLES) if f not in PICKED]
PLACE = {f: 1 + n for n, f in enumerate(GATHERED + PICKED)}
UNIT = 4
UNITS = [GATHERED[n:n + UNIT] for n in range(0, len(GATHERED), UNIT)]
NU = len(UNITS)
PARTS = 8
PART_ROWS = PICKED_ROWS // PARTS
DUO = 2
DUOS = len(PICKED) // DUO
PICKS = DUOS * PARTS
RING = 8

SHIFTS = (FEATURES - 1) // 2
PAIR_TILES = 3
PAIR_F = FEATURES // PAIR_TILES
PAIR_ROWS = SHIFTS * PAIR_F
WRAP_F = FEATURES - SHIFTS

H1_TILES, H2_TILES = HID1 // P, HID2 // P
ACCS = H1_TILES + H2_TILES + 1
LAST_K = [PAIR_TILES] * H1_TILES + [H1_TILES - 1] * H2_TILES + [H2_TILES - 1]
MLP_ITEMS = [(acc, k) for acc in range(ACCS) for k in range(LAST_K[acc] + 1)]


def share(items, steps, n):
    return items[len(items) * n // steps:len(items) * (n + 1) // steps] if 0 <= n < steps else []


def merge(*lists):
    keyed = [((n + 0.5) / len(x), i, v) for i, x in enumerate(lists) for n, v in enumerate(x)]
    return [v for _, _, v in sorted(keyed, key=lambda k: k[:2])]


def events(t_odd, u):
    batches = [("gram", b) for b in range(GRAM_BATCHES)]
    if t_odd:
        grams, others = share(batches, NU - 2, u - 2), share([("pick", n) for n in range(PICKS)], NU, u)
    else:
        grams, others = share(batches, NU, u), share([("mlp", m) for m in MLP_ITEMS], NU, u)
    return [("unit", u)] + merge(grams, others)


def first_events(u):
    return [("unit", u)] + share([("pick", n) for n in range(PICKS)], NU, u)


def steps(emit, lap, tiles):
    for j in tiles:
        t = LAP_TILES * lap + j if isinstance(lap, int) else None
        for u in range(NU):
            for kind, which in first_events(u) if t == 0 else events(j % 2, u):
                started = kind != "mlp" or t not in (1, 2)
                ended = kind == "pick" and t == TILES - 1
                if started and not ended:
                    emit(kind, which, lap, j)


def gram_tile(lap, j):
    return (lap, j - 1) if j else (lap - 1, LAP_TILES - 1)


def mlp_chunk(lap, j):
    return 2 * lap + j // 2 - 2


def pick_chunk(lap, j):
    return 2 * lap + (j + 1) // 2, (j + 1) // 2 % 2


def build(nc, ids, picked_ids, x_t, tables, w_pairs, w_dense_a, w_dense_b, b1, w2, b2, w3, eye, row_of, out):
    ids_t = ids.rearrange("(t p) f -> t p f", p=P)
    picked_ids_c = picked_ids.rearrange("(u a) (c m) -> c u a m", a=DUO, m=CHUNK)
    x_tiles = x_t.rearrange("d (t p) -> t d p", p=TILE)
    x_chunks = x_t.rearrange("d (c n) -> c d n", n=CHUNK)
    out_v = out.rearrange("(c j s q) o -> c o s j q", j=CHUNK_TILES, s=MEMBERS, q=GROUPS)
    scratch = nc.dram_tensor("gram_scratch", [2, FEATURES + SHIFTS, MEMBERS, FEATURES, CHUNK_GROUPS], F32).ap()

    with ExitStack() as ctx:
        def sb(name, shape, dt=F32):
            return ctx.enter_context(nc.sbuf_tensor(name, shape, dt))

        def pb(name):
            return ctx.enter_context(nc.psum_tensor(name, [P, 512], F32))

        def sem(name):
            return ctx.enter_context(nc.semaphore(name))

        index = sb("index", [P, LAP_TILES, TABLES], I32)
        rows = sb("rows", [P, 2, len(GATHERED), DIM])
        x_tile = sb("x_tile", [P, LAP_TILES, TILE])
        emb = sb("emb", [P, LAP_TILES, GROUPS, MEMBERS, FEATURES])
        raw_tables = emb[0:PART_ROWS, 2:4].rearrange("p j q s f -> p (j q s f)")[
            :, 0:len(PICKED) * PARTS * DIM].rearrange("p (n r) -> p n r", n=len(PICKED))
        halves = sb("halves", [PART_ROWS, 2, len(PICKED), PARTS * DIM], F32R)
        row_sb = sb("row_sb", [PART_ROWS, PARTS])
        picked_ids_sb = sb("picked_ids_sb", [PART_ROWS, DUOS, DUO * CHUNK], I32)
        one_hot = sb("one_hot", [PART_ROWS, RING, DUO * CHUNK], F32R)
        gram = sb("gram", [GROUP_COLS, GROUP_COLS, CHUNK_GROUPS])
        pairs = sb("pairs", [PAIR_ROWS, PAIR_TILES, MEMBERS, CHUNK_GROUPS])
        x_mlp = sb("x_mlp", [P, CHUNK])
        wp_sb = sb("wp_sb", [PAIR_ROWS, PAIR_TILES, HID1])
        wx_sb = sb("wx_sb", [P, HID1])
        wxb_sb = sb("wxb_sb", [P, HID1])
        w2_sb = sb("w2_sb", [P, H1_TILES, HID2])
        w3_sb = sb("w3_sb", [P, H2_TILES])
        b1_sb = sb("b1_sb", [P, H1_TILES])
        b2_sb = sb("b2_sb", [P, H2_TILES])
        eye_sb = sb("eye_sb", [P, P])
        h1 = sb("h1", [P, H1_TILES, CHUNK])
        h2 = sb("h2", [P, H2_TILES, CHUNK])
        y_row = sb("y_row", [1, CHUNK])

        unit_ps = [pb(f"unit_ps{i}") for i in range(2)]
        gram_ps = [pb(f"gram_ps{i}") for i in range(2)]
        mlp_ps = [pb(f"mlp_ps{i}") for i in range(2)]
        duo_ps = [pb(f"duo_ps{i}") for i in range(2)]

        index_in = [sem(f"index_in{i}") for i in range(LAP_TILES)]
        x_in = [sem(f"x_in{i}") for i in range(LAP_TILES)]
        picked_in = [sem(f"picked_in{i}") for i in range(DUOS)]
        gathered = [[sem(f"gathered{i}_{u}") for u in range(NU)] for i in range(2)]
        table_in = [sem(f"table_in{n}") for n in range(len(PICKED))]
        high_split, low_split = sem("high_split"), sem("low_split")
        weights_in, row_in, eye_in = sem("weights_in"), sem("row_in"), sem("eye_in")
        dense_summed = sem("dense_summed")
        x_placed = sem("x_placed")
        unit_ready, unit_taken = sem("unit_ready"), sem("unit_taken")
        one_hot_ready, one_hot_used, duo_taken = sem("one_hot_ready"), sem("one_hot_used"), sem("duo_taken")
        gram_ready, gram_taken = sem("gram_ready"), sem("gram_taken")
        scratch_out = [sem(f"scratch_out{s}") for s in range(MEMBERS)]
        mlp_in, mlp_ready = sem("mlp_in"), sem("mlp_ready")
        h1_taken, h2_taken, y_taken, y_out = sem("h1_taken"), sem("h2_taken"), sem("y_taken"), sem("y_out")
        gram_left = sem("gram_left")
        units_opened, loads_opened = sem("units_opened"), sem("loads_opened")

        WEIGHT_DMAS, MLP_DMAS = 7, MEMBERS * PAIR_TILES + 1

        def emb_place(j, place, n):
            return emb[:, j, :, :, place:place + n].rearrange("d q s f -> d f s q")

        def number(lap, j):
            return LAP_TILES * lap + j

        def early(lap, j, tiles):
            return isinstance(lap, int) and number(lap, j) < tiles

        block = ctx.enter_context(nc.Block())

        @block.sync
        def _(sp):
            def load_tile(lap, j):
                t = number(lap, j)
                if not early(lap, j, LAP_TILES):
                    sp.wait_ge(unit_ready, NU * (t - LAP_TILES + 1))
                    sp.sem_inc(loads_opened, 1)
                sp.dma_start(index[:, j, :], ids_t[t]).then_inc(index_in[j], 16)
                if not early(lap, j, LAP_TILES):
                    sp.wait_ge(x_placed, t - LAP_TILES + 1)
                    sp.sem_inc(loads_opened, 1)
                sp.dma_start(x_tile[:, j, :], x_tiles[t]).then_inc(x_in[j], 16)

            def load_picked_ids(c):
                if not (isinstance(c, int) and c == 0):
                    sp.wait_ge(one_hot_ready, PICKS * c)
                    sp.sem_inc(loads_opened, 1)
                for duo in range(DUOS):
                    sp.dma_start(picked_ids_sb[:, duo, :].rearrange("p (a m) -> p a m", a=DUO),
                                  picked_ids_c[c][duo].unsqueeze(0).broadcast_to([PART_ROWS, DUO, CHUNK])
                                  ).then_inc(picked_in[duo], 16)

            def bounce(c, i, last=False):
                sp.wait_ge(gram_taken, GRAM_BATCHES * CHUNK_TILES * (c + 1))
                sp.sem_inc(loads_opened, 1)
                for s in range(MEMBERS):
                    r = FEATURES * s
                    own = gram[r:r + FEATURES, r:r + FEATURES, :]
                    wrapped = gram[r:r + SHIFTS, r + WRAP_F:r + FEATURES, :]
                    sp.dma_start(scratch[i, 0:FEATURES, s, :, :], own).then_inc(scratch_out[s], 16)
                    sp.dma_start(scratch[i, FEATURES:FEATURES + SHIFTS, s, WRAP_F:, :],
                                 wrapped).then_inc(scratch_out[s], 16)
                sp.wait_ge(h1_taken, H1_TILES * c + 1)
                sp.sem_inc(loads_opened, 1)
                sp.dma_start(x_mlp[:, :], x_chunks[c]).then_inc(mlp_in, 16)
                if not last:
                    for s in range(MEMBERS):
                        sp.wait_ge(scratch_out[s], 32 * (c + 1))
                    sp.sem_inc(gram_left, 1)
                row = MEMBERS * FEATURES * CHUNK_GROUPS
                for s in range(MEMBERS):
                    if last:
                        sp.wait_ge(scratch_out[s], 32 * (c + 1))
                    for k in range(PAIR_TILES):
                        first = scratch[i, 1 + PAIR_F * k, s, PAIR_F * k, :]
                        src = bass.AP(tensor=first.tensor, offset=first.offset,
                                      ap=[[row, SHIFTS], [row + CHUNK_GROUPS, PAIR_F], [1, CHUNK_GROUPS]])
                        sp.dma_start(pairs[:, k, s], src).then_inc(mlp_in, 16)
                sp.wait_ge(mlp_in, 16 * MLP_DMAS * (c + 1))
                sp.sem_inc(loads_opened, 1)

            load_tile(0, 0)
            load_picked_ids(0)
            for n, f in enumerate(PICKED):
                sp.dma_start(raw_tables[:, n, :], tables[f].rearrange("(p r) d -> p (r d)", r=PARTS)
                             ).then_inc(table_in[n], 16)
                if n == 0:
                    sp.dma_start(eye_sb[:, :], eye).then_inc(eye_in, 16)
                    load_tile(0, 1)
            load_tile(0, 2)
            load_tile(0, 3)
            load_picked_ids(1)
            with sp.Fori(1, LAPS) as lap:
                load_tile(lap, 0)
                load_tile(lap, 1)
                load_picked_ids(2 * lap)
                bounce(2 * lap - 2, 0)
                load_tile(lap, 2)
                load_tile(lap, 3)
                load_picked_ids(2 * lap + 1)
                bounce(2 * lap - 1, 1)
            bounce(CHUNKS - 2, 0)
            bounce(CHUNKS - 1, 1, last=True)

        @block.gpsimd
        def _(pool):
            def gather_tile(lap, j):
                i = j % 2
                pool.wait_ge(index_in[j], 16 * (lap + 1))
                pool.sem_inc(units_opened, 1)
                for u, unit in enumerate(UNITS):
                    if not early(lap, j, 2):
                        pool.wait_ge(unit_ready, NU * (number(lap, j) - 2) + u + 1)
                        pool.sem_inc(units_opened, 1)
                    for f in unit:
                        nc.gpsimd.indirect_dma_start(
                            out=rows[:, i, PLACE[f] - 1, :], out_offset=None, in_=tables[f],
                            in_offset=bass.IndirectOffsetOnAxis(ap=index[:, j, f:f + 1], axis=0),
                        ).then_inc(gathered[i][u], 16)

            for j in range(LAP_TILES):
                gather_tile(0, j)
            with pool.Fori(1, LAPS) as lap:
                for j in range(LAP_TILES):
                    gather_tile(lap, j)

        def mlp_operands(acc, k):
            if acc < H1_TILES:
                m = slice(acc * P, (acc + 1) * P)
                if k < PAIR_TILES:
                    return wp_sb[:, k, m], pairs[:, k, :, :]
                return wx_sb[:, m], x_mlp[:, :].rearrange("d (j s q) -> d s j q", j=CHUNK_TILES, s=MEMBERS)
            if acc < H1_TILES + H2_TILES:
                m = acc - H1_TILES
                return w2_sb[:, k, m * P:(m + 1) * P], h1[:, k, :]
            return w3_sb[:, k:k + 1], h2[:, k, :]

        @block.tensor
        def _(pe):
            def unit(lap, j, u):
                i, n = j % 2, NU * number(lap, j) + u
                pe.wait_ge(gathered[i][u], 16 * UNIT * (2 * lap + j // 2 + 1))
                if not (isinstance(lap, int) and n < 2):
                    pe.wait_ge(unit_taken, n - 1)
                for a, f in enumerate(UNITS[u]):
                    last = nc.tensor.transpose(unit_ps[(j + u) % 2][:, a * TILE:(a + 1) * TILE],
                                               rows[:, i, PLACE[f] - 1, :], eye_sb[:, :])
                last.then_inc(unit_ready, 1)

            def gram_batch(lap, j, b):
                if b == 0:
                    pe.wait_ge(unit_taken, NU * (number(lap, j) + 1))
                    pe.wait_ge(x_placed, number(lap, j) + 1)
                    pe.wait_ge(duo_taken, DUOS * (2 * lap + j // 2 + 1))
                n = GRAM_BATCHES * number(lap, j) + b
                if not (isinstance(lap, int) and n < 2):
                    pe.wait_ge(gram_taken, n - 1)
                for a in range(BATCH_GROUPS):
                    q = b * BATCH_GROUPS + a
                    group = emb[:, j, q, :, :].rearrange("d s f -> d (s f)")
                    last = nc.tensor.matmul(gram_ps[b % 2][0:GROUP_COLS, a * GROUP_COLS:(a + 1) * GROUP_COLS],
                                            group, group, start=True, stop=True)
                last.then_inc(gram_ready, 1)

            def pick(c, i, n):
                duo, part = divmod(n, PARTS)
                if part == 0:
                    if isinstance(c, int) and c == 0:
                        pe.wait_ge(low_split, DUO * (duo + 1))
                    if not (isinstance(c, int) and DUOS * c + duo < 2):
                        pe.wait_ge(duo_taken, DUOS * c + duo - 1)
                pe.wait_ge(one_hot_ready, PICKS * c + n + 1)
                for a in range(DUO):
                    for half in range(2):
                        last = nc.tensor.matmul(
                            duo_ps[(i + duo) % 2][:, a * CHUNK:(a + 1) * CHUNK],
                            halves[:, half, duo * DUO + a, part * DIM:(part + 1) * DIM],
                            one_hot[:, n % RING, a * CHUNK:(a + 1) * CHUNK],
                            start=(part == 0 and a == 0 and half == 0),
                            stop=(part == PARTS - 1 and a == DUO - 1 and half == 1), skip_group_check=True)
                last.then_inc(one_hot_used, 1)

            def mlp_item(c, acc, k):
                if acc == 0 and k == 0:
                    pe.wait_ge(mlp_in, 16 * MLP_DMAS * (c + 1))
                    pe.wait_ge(y_taken, c + 1)
                if acc == 1 and k == 0:
                    pe.wait_ge(h2_taken, H2_TILES * c + 1)
                if 2 <= acc < H1_TILES and k == 0:
                    pe.wait_ge(h1_taken, H1_TILES * c + acc)
                if acc == H1_TILES and k == 0:
                    pe.wait_ge(h1_taken, H1_TILES * (c + 1) + 1)
                if acc == ACCS - 1 and k == 0:
                    pe.wait_ge(h2_taken, H2_TILES * (c + 1) + 1)
                lhs, rhs = mlp_operands(acc, k)
                o = mlp_ps[acc % 2][0:(1 if acc == ACCS - 1 else P), 0:CHUNK]
                mm = nc.tensor.matmul(o, lhs, rhs, start=(k == 0), stop=(k == LAST_K[acc]))
                if k == LAST_K[acc]:
                    mm.then_inc(mlp_ready, 1)

            def emit(kind, which, lap, j):
                if kind == "unit":
                    unit(lap, j, which)
                elif kind == "gram":
                    gram_batch(*gram_tile(lap, j), which)
                elif kind == "pick":
                    pick(*pick_chunk(lap, j), which)
                else:
                    mlp_item(mlp_chunk(lap, j), *which)

            pe.sem_inc(gram_ready, 1)
            pe.wait_ge(eye_in, 16)
            steps(emit, 0, range(3))
            pe.wait_ge(weights_in, 16 * WEIGHT_DMAS)
            pe.wait_ge(dense_summed, 1)
            with pe.Fori(1, LAPS) as lap:
                steps(emit, lap - 1, [3])
                steps(emit, lap, range(3))
            steps(emit, LAPS - 1, [3])
            for b in range(GRAM_BATCHES):
                gram_batch(LAPS - 1, LAP_TILES - 1, b)
            for c in (CHUNKS - 2, CHUNKS - 1):
                for acc, k in MLP_ITEMS:
                    mlp_item(c, acc, k)

        @block.scalar
        def _(act):
            for started, n in ((h1_taken, 1), (h2_taken, 1), (y_taken, 1), (y_out, 16)):
                act.sem_inc(started, n)
            act.dma_start(row_sb[:, :], row_of).then_inc(row_in, 16)

            def place_x(lap, j):
                t = number(lap, j)
                if isinstance(lap, int) and t == 2:
                    act.wait_ge(low_split, len(PICKED))
                if not early(lap, j, 3):
                    act.wait_ge(gram_ready, GRAM_BATCHES * (t - 3) + 1)
                act.wait_ge(x_in[j], 16 * (lap + 1))
                nc.scalar.copy(emb_place(j, 0, 1)[:, 0],
                               x_tile[:, j, :].rearrange("d (s q) -> d s q", s=MEMBERS)).then_inc(x_placed, 1)

            def take_unit(lap, j, u):
                act.wait_ge(unit_ready, NU * number(lap, j) + u + 1)
                src = unit_ps[(j + u) % 2][:, :].rearrange("d (f s q) -> d f s q", f=UNIT, s=MEMBERS)
                nc.scalar.copy(emb_place(j, PLACE[UNITS[u][0]], UNIT), src).then_inc(unit_taken, 1)

            def take_batch(lap, j, b):
                if b == 0 and j % 2 == 0 and not early(lap, j, 2):
                    act.wait_ge(gram_left, 2 * lap + j // 2)
                act.wait_ge(gram_ready, GRAM_BATCHES * number(lap, j) + b + 2)
                g0 = (j % 2) * GROUPS + b * BATCH_GROUPS
                src = gram_ps[b % 2][0:GROUP_COLS, 0:BATCH_GROUPS * GROUP_COLS].rearrange(
                    "r (q n) -> r n q", q=BATCH_GROUPS)
                nc.scalar.copy(gram[:, :, g0:g0 + BATCH_GROUPS], src).then_inc(gram_taken, 1)

            def take_duo(c, i, duo):
                act.wait_ge(one_hot_used, PARTS * (DUOS * c + duo + 1))
                if not (isinstance(c, int) and c < 2):
                    act.wait_ge(gram_ready, GRAM_BATCHES * CHUNK_TILES * (c - 1) + 1)
                for a in range(CHUNK_TILES):
                    src = duo_ps[(i + duo) % 2][:, :].rearrange("d (f j s q) -> d f j s q", f=DUO, j=CHUNK_TILES, s=MEMBERS)[:, :, a]
                    last = nc.scalar.copy(emb_place(CHUNK_TILES * i + a, PLACE[PICKED[duo * DUO]], DUO), src)
                last.then_inc(duo_taken, 1)

            def take_acc(c, acc):
                act.wait_ge(mlp_ready, ACCS * c + acc + 1)
                if acc < H1_TILES:
                    nc.scalar.activation(h1[:, acc, :], mlp_ps[acc % 2][:, 0:CHUNK], ACT.Relu,
                                         bias=b1_sb[:, acc:acc + 1]).then_inc(h1_taken, 1)
                elif acc < ACCS - 1:
                    m = acc - H1_TILES
                    nc.scalar.activation(h2[:, m, :], mlp_ps[acc % 2][:, 0:CHUNK], ACT.Relu,
                                         bias=b2_sb[:, m:m + 1]).then_inc(h2_taken, 1)
                else:
                    act.wait_ge(y_out, 16 * (c + 1))
                    nc.scalar.copy(y_row[:, :], mlp_ps[acc % 2][0:1, 0:CHUNK]).then_inc(y_taken, 1)
                    act.wait_ge(y_taken, c + 2)
                    act.dma_start(out_v[c], y_row[:, :].rearrange("o (s j q) -> o s j q", s=MEMBERS,
                                                                  j=CHUNK_TILES)).then_inc(y_out, 16)

            def emit(kind, which, lap, j):
                if kind == "unit":
                    if which == 0:
                        place_x(lap, j)
                    take_unit(lap, j, which)
                elif kind == "gram":
                    take_batch(*gram_tile(lap, j), which)
                elif kind == "pick" and which % PARTS == PARTS - 1:
                    take_duo(*pick_chunk(lap, j), which // PARTS)
                elif kind == "mlp" and which[1] == LAST_K[which[0]]:
                    take_acc(mlp_chunk(lap, j), which[0])

            for n in range(len(PICKED)):
                act.wait_ge(table_in[n], 16)
                nc.scalar.copy(halves[:, 0, n, :], raw_tables[:, n, :]).then_inc(high_split, 1)
            for dst, src in ((wp_sb, w_pairs), (wx_sb, w_dense_a), (wxb_sb, w_dense_b), (w2_sb, w2),
                             (w3_sb, w3), (b1_sb, b1), (b2_sb, b2)):
                act.dma_start(dst[:], src).then_inc(weights_in, 16)
            steps(emit, 0, range(3))
            act.wait_ge(weights_in, 16 * WEIGHT_DMAS)
            with act.Fori(1, LAPS) as lap:
                steps(emit, lap - 1, [3])
                steps(emit, lap, range(3))
            steps(emit, LAPS - 1, [3])
            for b in range(GRAM_BATCHES):
                take_batch(LAPS - 1, LAP_TILES - 1, b)
            for c in (CHUNKS - 2, CHUNKS - 1):
                for acc in range(ACCS):
                    take_acc(c, acc)
            act.wait_ge(y_out, 16 * (CHUNKS + 1))

        @block.vector
        def _(dve):
            def build_one_hots(c, picks=range(PICKS)):
                for n in picks:
                    duo, part = divmod(n, PARTS)
                    if part == 0:
                        dve.wait_ge(picked_in[duo], 16 * (c + 1))
                    if not (isinstance(c, int) and PICKS * c + n < RING):
                        dve.wait_ge(one_hot_used, PICKS * c + n + 1 - RING)
                    nc.vector.tensor_scalar(one_hot[:, n % RING, :], picked_ids_sb[:, duo, :],
                                            row_sb[:, part:part + 1], None, ALU.is_equal).then_inc(one_hot_ready, 1)

            def split(duo):
                for n in range(duo * DUO, (duo + 1) * DUO):
                    dve.wait_ge(high_split, n + 1)
                    nc.vector.tensor_tensor(halves[:, 1, n, :], raw_tables[:, n, :],
                                            halves[:, 0, n, :].bitcast(F32), ALU.subtract).then_inc(low_split, 1)

            dve.wait_ge(row_in, 16)
            build_one_hots(0, range(RING))
            for duo in range(DUOS):
                split(duo)
            build_one_hots(0, range(RING, PICKS))
            dve.wait_ge(weights_in, 16 * WEIGHT_DMAS)
            nc.vector.tensor_tensor(wx_sb[:, :], wx_sb[:, :], wxb_sb[:, :], ALU.add).then_inc(dense_summed, 1)
            with dve.Fori(1, CHUNKS) as c:
                build_one_hots(c)


def pair_rows():
    feature_at = [0] + [1 + f for f in GATHERED + PICKED]
    index = {}
    for i in range(FEATURES):
        for j in range(i + 1, FEATURES):
            index[i, j] = len(index)
    found = np.zeros((PAIR_ROWS, PAIR_TILES), np.int64)
    for k in range(PAIR_TILES):
        for d in range(SHIFTS):
            for n in range(PAIR_F):
                f = PAIR_F * k + n
                a, b = feature_at[f], feature_at[(f + d + 1) % FEATURES]
                found[d * PAIR_F + n, k] = index[min(a, b), max(a, b)]
    return found


def kernel(**inputs):
    import concourse.bacc as bacc
    from concourse.bass_utils import run_bass_kernel_spmd

    a = {k: np.ascontiguousarray(v) for k, v in inputs.items()}
    w1 = a["W_top1"]
    arrays = {
        "ids": a["ids"],
        "picked_ids": np.ascontiguousarray(a["ids"][:, PICKED].T),
        "x_t": np.ascontiguousarray(a["r_dense_features"].T),
        "w_pairs": np.ascontiguousarray(w1[DIM:DIM + PAIRS][pair_rows()]),
        "w_dense_a": np.ascontiguousarray(w1[:DIM]),
        "w_dense_b": np.ascontiguousarray(w1[DIM + PAIRS:]),
        "b1": np.ascontiguousarray(a["b_top1"].reshape(H1_TILES, P).T),
        "w2": np.ascontiguousarray(a["W_top2"].reshape(H1_TILES, P, HID2).transpose(1, 0, 2)),
        "b2": np.ascontiguousarray(a["b_top2"].reshape(H2_TILES, P).T),
        "w3": np.ascontiguousarray(a["W_top3"].reshape(H2_TILES, P).T),
        "eye": np.eye(P, dtype=np.float32),
        "row_of": np.arange(PICKED_ROWS, dtype=np.float32).reshape(PART_ROWS, PARTS),
    }
    for f in range(TABLES):
        arrays[f"tbl_{f}"] = a[f"tbl_{f}"]
    nc = bacc.Bacc("TRN2", target_bir_lowering=False, num_devices=1)
    ap = {k: nc.dram_tensor(k, v.shape, mybir.dt.from_np(v.dtype), kind="ExternalInput").ap()
          for k, v in arrays.items()}
    out = nc.dram_tensor("y", (BATCH, 1), F32, kind="ExternalOutput").ap()
    build(nc, ap["ids"], ap["picked_ids"], ap["x_t"], [ap[f"tbl_{f}"] for f in range(TABLES)], ap["w_pairs"], ap["w_dense_a"],
          ap["w_dense_b"], ap["b1"], ap["w2"], ap["b2"], ap["w3"], ap["eye"], ap["row_of"], out)
    r = run_bass_kernel_spmd(nc, [arrays], core_ids=[0])
    return r.results[0]["y"]
```

```python
import numpy as np
import concourse.bass as bass
from concourse import mybir
from contextlib import ExitStack

F32 = mybir.dt.float32
F32R = mybir.dt.float32r
I32 = mybir.dt.int32
ACT = mybir.ActivationFunctionType
ALU = mybir.AluOpType

BATCH, DIM, TABLES = 2048, 128, 26
FEATURES = TABLES + 1
HID1, HID2 = 512, 256
PAIRS = FEATURES * (FEATURES - 1) // 2

P = 128
TILE, CHUNK_TILES, LAP_TILES = P, 2, 4
TILES = BATCH // TILE
CHUNK = TILE * CHUNK_TILES
CHUNKS = BATCH // CHUNK
LAPS = TILES // LAP_TILES
MEMBERS, GROUPS = 4, TILE // 4
CHUNK_GROUPS = GROUPS * CHUNK_TILES
GROUP_COLS = MEMBERS * FEATURES
BATCH_GROUPS = 4
GRAM_BATCHES = GROUPS // BATCH_GROUPS

PART_ROWS = 125
TURNS = [([8, 9], 8), ([10, 13], 8), ([19, 21], 8), ([0], 10)]
PICKED = [f for of_turn, _ in TURNS for f in of_turn]
PARTS_OF = {f: parts for of_turn, parts in TURNS for f in of_turn}
GATHERED = [f for f in range(TABLES) if f not in PICKED]
PLACE = {f: 1 + n for n, f in enumerate(GATHERED + PICKED)}
UNIT = 4
UNITS = [GATHERED[n:n + UNIT] for n in range(0, len(GATHERED), UNIT)]
NU = len(UNITS)
NT = len(TURNS)
MOST = max(len(of_turn) for of_turn, _ in TURNS)
PICK_ITEMS = [(turn, part) for turn, (_, parts) in enumerate(TURNS) for part in range(parts)]
PICKS = len(PICK_ITEMS)
PICK_END = [sum(parts for _, parts in TURNS[:turn + 1]) for turn in range(NT)]
PART_KINDS = sorted(set(PARTS_OF.values()))
RING = 3
PART_AT = {f: sum(PARTS_OF[g] for g in PICKED[:n]) for n, f in enumerate(PICKED)}
ALL_PARTS = sum(PARTS_OF[f] for f in PICKED)

SHIFTS = (FEATURES - 1) // 2
PAIR_TILES = 3
PAIR_F = FEATURES // PAIR_TILES
PAIR_ROWS = SHIFTS * PAIR_F
WRAP_F = FEATURES - SHIFTS

H1_TILES, H2_TILES = HID1 // P, HID2 // P
ACCS = H1_TILES + H2_TILES + 1
LAST_K = [PAIR_TILES] * H1_TILES + [H1_TILES - 1] * H2_TILES + [H2_TILES - 1]
MLP_ITEMS = [(acc, k) for acc in range(ACCS) for k in range(LAST_K[acc] + 1)]


SHIFTED, BEGUN = 24, 4
TAIL_CUTS = (8, 12, 12)
FIRST_CUTS = dict(pick=[0, 7, 14, 21, 28, PICKS])
SECOND_CUTS = dict(gram=[0, 4, 8, 8, 8, GRAM_BATCHES], pick=[0, 4, 11, 18, 26, PICKS])
LATER_CUTS = [dict(gram=[0, 1, 3, 4, 6, GRAM_BATCHES], mlp=[0, 5, 10, 15, 20, SHIFTED]),
              dict(gram=[0, 0, 0, 2, 5, GRAM_BATCHES], pick=[0, 6, 13, 20, 27, PICKS],
                   mlp=[SHIFTED] + [len(MLP_ITEMS)] * 5),
              dict(gram=[0, 2, 4, 6, 7, GRAM_BATCHES], mlp=[0, 5, 9, 13, 19, len(MLP_ITEMS)]),
              dict(gram=[0, 0, 0, 2, 5, GRAM_BATCHES], pick=[0, 6, 13, 20, 27, PICKS])]
LAST_CUTS = dict(gram=[0, 3, 6, 8, 8, GRAM_BATCHES], mlp=[0, 0, 0, 0, BEGUN, BEGUN])


def merge(*lists):
    keyed = [((n + 0.5) / len(x), i, v) for i, x in enumerate(lists) for n, v in enumerate(x)]
    return [v for _, _, v in sorted(keyed, key=lambda k: k[:2])]


def tail_events():
    left = [("mlp", m) for m in MLP_ITEMS[BEGUN:]]
    tiles = [[(("tile", tile), m) for m in MLP_ITEMS] for tile in range(CHUNK_TILES)]
    a, b, c = TAIL_CUTS
    return (merge([("gram", n) for n in range(GRAM_BATCHES)], left[:a]) + merge(left[a:], tiles[0][:b])
            + merge(tiles[0][b:], tiles[1][:c]) + tiles[1][c:])


def events(t, j, u):
    cuts = (FIRST_CUTS if t == 0 else SECOND_CUTS if t == 1 else LAST_CUTS if t == TILES - 1
            else LATER_CUTS[j])
    items = dict(gram=range(GRAM_BATCHES), pick=range(PICKS), mlp=MLP_ITEMS)
    return [("unit", u)] + merge(*([(kind, n) for n in items[kind][at[u]:at[u + 1]]] for kind, at in cuts.items()))


def steps(emit, lap, tiles):
    for j in tiles:
        t = LAP_TILES * lap + j if isinstance(lap, int) else None
        for u in range(NU):
            for kind, which in events(t, j, u):
                if kind != "mlp" or t != 2:
                    emit(kind, which, lap, j)


def gram_tile(lap, j):
    return (lap, j - 1) if j else (lap - 1, LAP_TILES - 1)


def mlp_chunk(lap, j):
    return 2 * lap - 2 + (j // 2 if j < LAP_TILES - 1 else CHUNK_TILES)


def pick_chunk(lap, j):
    return 2 * lap + (j + 1) // 2, (j + 1) // 2 % 2


def build(nc, ids, picked_ids, x_t, tables, w_pairs, w_dense_a, w_dense_b, b1, w2, b2, w3, eye, row_of, out):
    ids_t = ids.rearrange("(t p) f -> t p f", p=P)
    picked_ids_c = picked_ids.rearrange("n (c m) -> c n m", m=CHUNK)
    x_tiles = x_t.rearrange("d (t p) -> t d p", p=TILE)
    x_chunks = x_t.rearrange("d (c n) -> c d n", n=CHUNK)
    out_v = out.rearrange("(c j s q) o -> c o s j q", j=CHUNK_TILES, s=MEMBERS, q=GROUPS)
    out_tiles = out.rearrange("(t p) o -> t o p", p=TILE)
    scratch = nc.dram_tensor("gram_scratch", [2, FEATURES + SHIFTS, FEATURES, MEMBERS, CHUNK_GROUPS], F32).ap()
    last_scratch = nc.dram_tensor("last_scratch", [CHUNK_TILES, FEATURES + SHIFTS, FEATURES, MEMBERS, GROUPS],
                                  F32).ap()

    with ExitStack() as ctx:
        def sb(name, shape, dt=F32):
            return ctx.enter_context(nc.sbuf_tensor(name, shape, dt))

        def pb(name):
            return ctx.enter_context(nc.psum_tensor(name, [P, 512], F32))

        def sem(name):
            return ctx.enter_context(nc.semaphore(name))

        index = sb("index", [P, LAP_TILES, TABLES], I32)
        rows = sb("rows", [P, 2, len(GATHERED), DIM])
        x_tile = sb("x_tile", [P, 2, TILE])
        emb = sb("emb", [P, LAP_TILES, GROUPS, MEMBERS, FEATURES])
        halves = sb("halves", [PART_ROWS, 2, ALL_PARTS * DIM], F32R)
        row_sb = sb("row_sb", [PART_ROWS, len(PART_KINDS), max(PART_KINDS)])
        picked_ids_sb = sb("picked_ids_sb", [PART_ROWS, len(PICKED), CHUNK], I32)
        one_hot = sb("one_hot", [PART_ROWS, RING, MOST * CHUNK], F32R)
        gram = sb("gram", [GROUP_COLS, GROUP_COLS, CHUNK_GROUPS])
        pairs = sb("pairs", [PAIR_ROWS, PAIR_TILES, MEMBERS, CHUNK_GROUPS])
        x_mlp = sb("x_mlp", [P, CHUNK])
        pair_halves = sb("pair_halves", [PAIR_ROWS, 2, PAIR_TILES, CHUNK], F32R)
        wp_halves = sb("wp_halves", [PAIR_ROWS, 2, PAIR_TILES, HID1], F32R)
        wx_sb = sb("wx_sb", [P, HID1])
        w2_sb = sb("w2_sb", [P, H1_TILES, HID2])
        w3_sb = sb("w3_sb", [P, H2_TILES])
        b1_sb = sb("b1_sb", [P, H1_TILES])
        b2_sb = sb("b2_sb", [P, H2_TILES])
        eye_sb = sb("eye_sb", [P, P])
        h1 = sb("h1", [P, H1_TILES, CHUNK])
        h2 = sb("h2", [P, H2_TILES, CHUNK])
        y_row = h2[0:1, 0, :]

        spare = emb[:, 1:4].rearrange("p j q s f -> p (j q s f)")
        raw_tables = [spare[0:PART_ROWS, PART_AT[f] * DIM:(PART_AT[f] + PARTS_OF[f]) * DIM] for f in PICKED]
        wxb_sb = spare[:, ALL_PARTS * DIM:ALL_PARTS * DIM + HID1]
        wp_at = ALL_PARTS * DIM + HID1
        wp_sb = spare[0:PAIR_ROWS, wp_at:wp_at + PAIR_TILES * HID1].rearrange("r (k n) -> r k n", k=PAIR_TILES)

        last_gram = [emb[0:GROUP_COLS, j].rearrange("r q s f -> r (q s f)").rearrange("r (n g) -> r n g", g=GROUPS)
                     for j in range(CHUNK_TILES)]
        rows_0 = rows[:, 0].rearrange("p n d -> p (n d)")
        last_wp = rows_0[0:PAIR_ROWS, 0:PAIR_TILES * HID1].rearrange("r (k n) -> r k n", k=PAIR_TILES)
        last_x = rows_0[:, PAIR_TILES * HID1:PAIR_TILES * HID1 + CHUNK]
        last_pairs = pairs[:].rearrange("r k s g -> r k (s g)")

        emb_2 = emb[:, 2].rearrange("p q s f -> p (q s f)")
        hidden_at = (H1_TILES + H2_TILES) * TILE
        last_hidden = [emb_2[:, j * hidden_at:(j + 1) * hidden_at].rearrange("p (m n) -> p m n", n=TILE)
                       for j in range(CHUNK_TILES)]
        last_y = [emb_2[0:1, CHUNK_TILES * hidden_at + j * TILE:CHUNK_TILES * hidden_at + (j + 1) * TILE]
                  for j in range(CHUNK_TILES)]

        unit_ps = [pb(f"unit_ps{i}") for i in range(2)]
        gram_ps = [pb(f"gram_ps{i}") for i in range(2)]
        mlp_ps = [pb(f"mlp_ps{i}") for i in range(2)]
        turn_ps = [pb(f"turn_ps{i}") for i in range(2)]

        index_in = [sem(f"index_in{i}") for i in range(LAP_TILES)]
        x_in = [sem(f"x_in{i}") for i in range(2)]
        picked_in = [sem(f"picked_in{i}") for i in range(NT)]
        gathered = [[sem(f"gathered{i}_{u}") for u in range(NU)] for i in range(2)]
        table_in = [sem(f"table_in{n}") for n in range(len(PICKED))]
        high_split, low_split = sem("high_split"), sem("low_split")
        weights_in, row_in, eye_in = sem("weights_in"), sem("row_in"), sem("eye_in")
        dense_summed = sem("dense_summed")
        x_placed = sem("x_placed")
        unit_ready, unit_taken = sem("unit_ready"), sem("unit_taken")
        one_hot_ready, one_hot_used, turn_taken = sem("one_hot_ready"), sem("one_hot_used"), sem("turn_taken")
        gram_ready, gram_taken = sem("gram_ready"), sem("gram_taken")
        scratch_out = sem("scratch_out")
        x_mlp_in, pairs_in = sem("x_mlp_in"), [sem(f"pairs_in{k}") for k in range(PAIR_TILES)]
        wp_split, pairs_high_split, pairs_split = sem("wp_split"), sem("pairs_high_split"), sem("pairs_split")
        mlp_ready, last_in = sem("mlp_ready"), sem("last_in")
        tile_ready = [sem(f"tile_ready{j}") for j in range(CHUNK_TILES)]
        tile_taken = [sem(f"tile_taken{j}") for j in range(CHUNK_TILES)]
        h1_taken, h2_taken, y_taken, y_out = sem("h1_taken"), sem("h2_taken"), sem("y_taken"), sem("y_out")
        gram_left = sem("gram_left")
        units_opened, loads_opened = sem("units_opened"), sem("loads_opened")

        WEIGHT_DMAS, SCRATCH_DMAS = 7, 2 * MEMBERS

        def emb_place(j, place, n):
            return emb[:, j, :, :, place:place + n].rearrange("d q s f -> d f s q")

        def number(lap, j):
            return LAP_TILES * lap + j

        def table_half(half, n):
            at = PART_AT[PICKED[n]] * DIM
            return halves[:, half, at:at + PARTS_OF[PICKED[n]] * DIM]

        def early(lap, j, tiles):
            return isinstance(lap, int) and number(lap, j) < tiles

        block = ctx.enter_context(nc.Block())

        @block.sync
        def _(sp):
            def load_index(lap, j):
                t = number(lap, j)
                if not early(lap, j, LAP_TILES):
                    sp.wait_ge(unit_ready, NU * (t - LAP_TILES + 1))
                    sp.sem_inc(loads_opened, 1)
                sp.dma_start(index[:, j, :], ids_t[t]).then_inc(index_in[j], 16)

            def load_x(lap, j):
                t = number(lap, j)
                if not early(lap, j, 2):
                    sp.wait_ge(x_placed, t - 1)
                    sp.sem_inc(loads_opened, 1)
                sp.dma_start(x_tile[:, j % 2, :], x_tiles[t]).then_inc(x_in[j % 2], 16)

            def load_picked_ids(c):
                if not (isinstance(c, int) and c == 0):
                    sp.wait_ge(one_hot_ready, PICKS * c)
                    sp.sem_inc(loads_opened, 1)
                for turn, (of_turn, _) in enumerate(TURNS):
                    n0 = PICKED.index(of_turn[0])
                    n1 = n0 + len(of_turn)
                    sp.dma_start(picked_ids_sb[:, n0:n1, :], picked_ids_c[c][n0:n1].unsqueeze(0).broadcast_to(
                        [PART_ROWS, n1 - n0, CHUNK])).then_inc(picked_in[turn], 16)

            def bounce(c, i):
                sp.wait_ge(gram_taken, GRAM_BATCHES * CHUNK_TILES * (c + 1))
                sp.sem_inc(loads_opened, 1)
                for s in range(MEMBERS):
                    r = FEATURES * s
                    own = gram[r:r + FEATURES, r:r + FEATURES, :]
                    wrapped = gram[r:r + SHIFTS, r + WRAP_F:r + FEATURES, :]
                    sp.dma_start(scratch[i, 0:FEATURES, :, s, :], own).then_inc(scratch_out, 16)
                    sp.dma_start(scratch[i, FEATURES:FEATURES + SHIFTS, WRAP_F:, s, :],
                                 wrapped).then_inc(scratch_out, 16)
                sp.wait_ge(h1_taken, H1_TILES * c + 1)
                sp.sem_inc(loads_opened, 1)
                sp.dma_start(x_mlp[:, :], x_chunks[c]).then_inc(x_mlp_in, 16)
                sp.wait_ge(scratch_out, 16 * SCRATCH_DMAS * (c + 1))
                sp.sem_inc(gram_left, 1)
                row = FEATURES * MEMBERS * CHUNK_GROUPS
                for k in range(PAIR_TILES):
                    first = scratch[i, 1 + PAIR_F * k, PAIR_F * k, 0, :]
                    src = bass.AP(tensor=first.tensor, offset=first.offset,
                                  ap=[[row, SHIFTS], [row + MEMBERS * CHUNK_GROUPS, PAIR_F],
                                      [1, MEMBERS * CHUNK_GROUPS]])
                    sp.dma_start(pairs[:, k].rearrange("r s g -> r (s g)"), src).then_inc(pairs_in[k], 16)
                for k in range(PAIR_TILES):
                    sp.wait_ge(pairs_in[k], 16 * (c + 1))
                sp.sem_inc(loads_opened, 1)

            def load_last():
                sp.wait_ge(unit_ready, NU * (TILES - 1))
                sp.dma_start(last_wp, w_pairs).then_inc(last_in, 16)
                sp.dma_start(last_x, x_chunks[CHUNKS - 1]).then_inc(last_in, 16)

            def bounce_tile(j):
                sp.wait_ge(gram_taken, GRAM_BATCHES * (TILES - CHUNK_TILES + j + 1))
                for s in range(MEMBERS):
                    r = FEATURES * s
                    own = last_gram[j][r:r + FEATURES, r:r + FEATURES, :]
                    wrapped = last_gram[j][r:r + SHIFTS, r + WRAP_F:r + FEATURES, :]
                    sp.dma_start(last_scratch[j, 0:FEATURES, :, s, :], own).then_inc(scratch_out, 16)
                    sp.dma_start(last_scratch[j, FEATURES:FEATURES + SHIFTS, WRAP_F:, s, :],
                                 wrapped).then_inc(scratch_out, 16)
                sp.wait_ge(scratch_out, 16 * SCRATCH_DMAS * (CHUNKS + j))
                sp.wait_ge(pairs_split, PAIR_TILES * (CHUNKS - 1))
                if j == 1:
                    for k in range(PAIR_TILES):
                        sp.wait_ge(pairs_in[k], 16 * CHUNKS)
                row = FEATURES * TILE
                for k in range(PAIR_TILES):
                    first = last_scratch[j, 1 + PAIR_F * k, PAIR_F * k, 0, :]
                    src = bass.AP(tensor=first.tensor, offset=first.offset,
                                  ap=[[row, SHIFTS], [row + TILE, PAIR_F], [1, TILE]])
                    sp.dma_start(last_pairs[:, k, j * TILE:(j + 1) * TILE], src).then_inc(pairs_in[k], 16)

            load_index(0, 0)
            load_x(0, 0)
            load_picked_ids(0)
            for n, f in enumerate(PICKED):
                sp.dma_start(raw_tables[n], tables[f].rearrange("(p r) d -> p (r d)", r=PARTS_OF[f])
                             ).then_inc(table_in[n], 16)
                if n == 0:
                    sp.dma_start(eye_sb[:, :], eye).then_inc(eye_in, 16)
                    load_index(0, 1)
                    load_x(0, 1)
            load_index(0, 2)
            load_index(0, 3)
            load_picked_ids(1)
            load_x(0, 2)
            load_x(0, 3)
            with sp.Fori(1, LAPS) as lap:
                load_index(lap, 0)
                load_index(lap, 1)
                load_picked_ids(2 * lap)
                bounce(2 * lap - 2, 0)
                load_x(lap, 0)
                load_x(lap, 1)
                load_index(lap, 2)
                load_index(lap, 3)
                load_picked_ids(2 * lap + 1)
                bounce(2 * lap - 1, 1)
                load_x(lap, 2)
                load_x(lap, 3)
            bounce(CHUNKS - 2, 0)
            load_last()
            for j in range(CHUNK_TILES):
                bounce_tile(j)

        @block.gpsimd
        def _(pool):
            def gather_tile(lap, j):
                i = j % 2
                pool.wait_ge(index_in[j], 16 * (lap + 1))
                pool.sem_inc(units_opened, 1)
                for u, unit in enumerate(UNITS):
                    if not early(lap, j, 2):
                        pool.wait_ge(unit_ready, NU * (number(lap, j) - 2) + u + 1)
                        pool.sem_inc(units_opened, 1)
                    for f in unit:
                        nc.gpsimd.indirect_dma_start(
                            out=rows[:, i, PLACE[f] - 1, :], out_offset=None, in_=tables[f],
                            in_offset=bass.IndirectOffsetOnAxis(ap=index[:, j, f:f + 1], axis=0),
                        ).then_inc(gathered[i][u], 16)

            for j in range(LAP_TILES):
                gather_tile(0, j)
            with pool.Fori(1, LAPS) as lap:
                for j in range(LAP_TILES):
                    gather_tile(lap, j)

        last_ps = [gram_ps, turn_ps]

        def mlp_operands(acc, k):
            if acc < H1_TILES:
                m = slice(acc * P, (acc + 1) * P)
                if k == 0:
                    return [(wx_sb[:, m], x_mlp[:, :].rearrange("d (j s q) -> d s j q", j=CHUNK_TILES, s=MEMBERS))]
                w_high, w_low = wp_halves[:, 0, k - 1, m], wp_halves[:, 1, k - 1, m]
                high, low = pair_halves[:, 0, k - 1, :], pair_halves[:, 1, k - 1, :]
                return [(w_high, high), (w_high, low), (w_low, high)]
            if acc < H1_TILES + H2_TILES:
                m = acc - H1_TILES
                return [(w2_sb[:, k, m * P:(m + 1) * P], h1[:, k, :])]
            return [(w3_sb[:, k:k + 1], h2[:, k, :])]

        def tile_operands(tile, acc, k):
            hidden = last_hidden[tile]
            if acc < H1_TILES:
                m, n = slice(acc * P, (acc + 1) * P), slice(tile * TILE, (tile + 1) * TILE)
                return (wx_sb[:, m], last_x[:, n]) if k == 0 else (last_wp[:, k - 1, m], last_pairs[:, k - 1, n])
            if acc < H1_TILES + H2_TILES:
                m = acc - H1_TILES
                return w2_sb[:, k, m * P:(m + 1) * P], hidden[:, k, :]
            return w3_sb[:, k:k + 1], hidden[:, H1_TILES + k, :]

        @block.tensor
        def _(pe):
            def unit(lap, j, u):
                i, n = j % 2, NU * number(lap, j) + u
                pe.wait_ge(gathered[i][u], 16 * len(UNITS[u]) * (2 * lap + j // 2 + 1))
                if not (isinstance(lap, int) and n < 2):
                    pe.wait_ge(unit_taken, n - 1)
                for a, f in enumerate(UNITS[u]):
                    last = nc.tensor.transpose(unit_ps[(j + u) % 2][:, a * TILE:(a + 1) * TILE],
                                               rows[:, i, PLACE[f] - 1, :], eye_sb[:, :])
                last.then_inc(unit_ready, 1)

            def gram_batch(lap, j, b):
                if b == 0:
                    pe.wait_ge(unit_taken, NU * (number(lap, j) + 1))
                    pe.wait_ge(x_placed, number(lap, j) + 1)
                    pe.wait_ge(turn_taken, NT * (2 * lap + j // 2 + 1))
                n = GRAM_BATCHES * number(lap, j) + b
                if not (isinstance(lap, int) and n < 2):
                    pe.wait_ge(gram_taken, n - 1)
                for a in range(BATCH_GROUPS):
                    q = b * BATCH_GROUPS + a
                    group = emb[:, j, q, :, :].rearrange("d s f -> d (s f)")
                    last = nc.tensor.matmul(gram_ps[b % 2][0:GROUP_COLS, a * GROUP_COLS:(a + 1) * GROUP_COLS],
                                            group, group, start=True, stop=True)
                last.then_inc(gram_ready, 1)

            def pick(c, n):
                turn, part = PICK_ITEMS[n]
                of_turn, parts = TURNS[turn]
                if part == 0:
                    if isinstance(c, int) and c == 0:
                        pe.wait_ge(low_split, PICKED.index(of_turn[-1]) + 1)
                    if not (isinstance(c, int) and NT * c + turn < 2):
                        pe.wait_ge(turn_taken, NT * c + turn - 1)
                pe.wait_ge(one_hot_ready, PICKS * c + n + 1)
                for a, f in enumerate(of_turn):
                    at = (PART_AT[f] + part) * DIM
                    for half in range(2):
                        last = nc.tensor.matmul(
                            turn_ps[turn % 2][:, a * CHUNK:(a + 1) * CHUNK], halves[:, half, at:at + DIM],
                            one_hot[:, n % RING, a * CHUNK:(a + 1) * CHUNK],
                            start=(part == 0 and a == 0 and half == 0),
                            stop=(part == parts - 1 and a == len(of_turn) - 1 and half == 1),
                            skip_group_check=True)
                last.then_inc(one_hot_used, 1)

            def mlp_item(c, acc, k):
                if acc == 0 and k == 0:
                    pe.wait_ge(x_mlp_in, 16 * (c + 1))
                    pe.wait_ge(y_taken, c + 1)
                if acc == 0 and k > 0:
                    pe.wait_ge(pairs_split, PAIR_TILES * c + k)
                if acc == 1 and k == 0:
                    pe.wait_ge(h2_taken, H2_TILES * c + 1)
                if 2 <= acc < H1_TILES and k == 0:
                    pe.wait_ge(h1_taken, H1_TILES * c + acc)
                if acc == H1_TILES and k == 0:
                    pe.wait_ge(h1_taken, H1_TILES * (c + 1) + 1)
                if acc == ACCS - 1 and k == 0:
                    pe.wait_ge(h2_taken, H2_TILES * (c + 1) + 1)
                o = mlp_ps[acc % 2][0:(1 if acc == ACCS - 1 else P), 0:CHUNK]
                products = mlp_operands(acc, k)
                for n, (lhs, rhs) in enumerate(products):
                    last = nc.tensor.matmul(o, lhs, rhs, start=(k == 0 and n == 0),
                                            stop=(k == LAST_K[acc] and n == len(products) - 1))
                if k == LAST_K[acc]:
                    last.then_inc(mlp_ready, 1)

            def tile_item(tile, acc, k):
                taken = tile_taken[tile]
                if acc == 0 and k == 0 and tile == 0:
                    pe.wait_ge(last_in, 32)
                    pe.wait_ge(gram_taken, GRAM_BATCHES * TILES)
                if acc == 0 and k == 0 and tile == 1:
                    pe.wait_ge(turn_taken, NT * CHUNKS)
                if acc == 0 and k > 0:
                    pe.wait_ge(pairs_in[k - 1], 16 * (CHUNKS + tile))
                if 2 <= acc < H1_TILES and k == 0:
                    pe.wait_ge(taken, acc - 1)
                if acc == H1_TILES and k == 0:
                    pe.wait_ge(taken, H1_TILES)
                if acc == ACCS - 1 and k == 0:
                    pe.wait_ge(taken, H1_TILES + H2_TILES)
                lhs, rhs = tile_operands(tile, acc, k)
                o = last_ps[tile][acc % 2][0:(1 if acc == ACCS - 1 else P), 0:TILE]
                last = nc.tensor.matmul(o, lhs, rhs, start=(k == 0), stop=(k == LAST_K[acc]))
                if k == LAST_K[acc]:
                    last.then_inc(tile_ready[tile], 1)

            def emit(kind, which, lap, j):
                if kind == "unit":
                    unit(lap, j, which)
                elif kind == "gram":
                    gram_batch(*gram_tile(lap, j), which)
                elif kind == "pick":
                    pick(pick_chunk(lap, j)[0], which)
                else:
                    mlp_item(mlp_chunk(lap, j), *which)

            pe.sem_inc(gram_ready, 1)
            pe.wait_ge(eye_in, 16)
            steps(emit, 0, range(3))
            pe.wait_ge(weights_in, 16 * WEIGHT_DMAS)
            pe.wait_ge(dense_summed, 1)
            pe.wait_ge(wp_split, 2)
            with pe.Fori(1, LAPS) as lap:
                steps(emit, lap - 1, [3])
                steps(emit, lap, range(3))
            steps(emit, LAPS - 1, [3])
            for kind, which in tail_events():
                if kind == "gram":
                    gram_batch(LAPS - 1, LAP_TILES - 1, which)
                elif kind == "mlp":
                    mlp_item(CHUNKS - 2, *which)
                else:
                    tile_item(kind[1], *which)

        @block.scalar
        def _(act):
            for started, n in ((h1_taken, 1), (h2_taken, 1), (y_taken, 1), (y_out, 16)):
                act.sem_inc(started, n)
            act.dma_start(row_sb[:], row_of).then_inc(row_in, 16)

            def place_x(lap, j):
                t = number(lap, j)
                if not early(lap, j, 3):
                    act.wait_ge(gram_ready, GRAM_BATCHES * (t - 3) + 1)
                act.wait_ge(x_in[j % 2], 16 * (2 * lap + j // 2 + 1))
                nc.scalar.copy(emb_place(j, 0, 1)[:, 0],
                               x_tile[:, j % 2, :].rearrange("d (s q) -> d s q", s=MEMBERS)).then_inc(x_placed, 1)

            def take_unit(lap, j, u):
                act.wait_ge(unit_ready, NU * number(lap, j) + u + 1)
                n = len(UNITS[u])
                src = unit_ps[(j + u) % 2][:, 0:n * TILE].rearrange("d (f s q) -> d f s q", f=n, s=MEMBERS)
                nc.scalar.copy(emb_place(j, PLACE[UNITS[u][0]], n), src).then_inc(unit_taken, 1)

            def take_batch(lap, j, b):
                last = isinstance(lap, int) and number(lap, j) >= TILES - CHUNK_TILES
                if b == 0 and j % 2 == 0 and not early(lap, j, 2) and not last:
                    act.wait_ge(gram_left, 2 * lap + j // 2)
                act.wait_ge(gram_ready, GRAM_BATCHES * number(lap, j) + b + 2)
                g0 = b * BATCH_GROUPS + (0 if last else (j % 2) * GROUPS)
                src = gram_ps[b % 2][0:GROUP_COLS, 0:BATCH_GROUPS * GROUP_COLS].rearrange(
                    "r (q n) -> r n q", q=BATCH_GROUPS)
                dst = last_gram[j % 2] if last else gram
                nc.scalar.copy(dst[:, :, g0:g0 + BATCH_GROUPS], src).then_inc(gram_taken, 1)

            def take_turn(c, i, turn):
                of_turn, _ = TURNS[turn]
                act.wait_ge(one_hot_used, PICKS * c + PICK_END[turn])
                if isinstance(c, int) and c == 0 and turn == 0:
                    act.wait_ge(low_split, len(PICKED))
                if isinstance(c, int) and c == 1 and turn == 0:
                    act.wait_ge(dense_summed, 1)
                    act.wait_ge(wp_split, 2)
                if not (isinstance(c, int) and c < 2):
                    act.wait_ge(gram_ready, GRAM_BATCHES * CHUNK_TILES * (c - 1) + 1)
                for a in range(CHUNK_TILES):
                    src = turn_ps[turn % 2][:, 0:len(of_turn) * CHUNK].rearrange(
                        "d (f j s q) -> d f j s q", f=len(of_turn), j=CHUNK_TILES, s=MEMBERS)[:, :, a]
                    last = nc.scalar.copy(emb_place(CHUNK_TILES * i + a, PLACE[of_turn[0]], len(of_turn)), src)
                last.then_inc(turn_taken, 1)

            def take_acc(c, acc):
                act.wait_ge(mlp_ready, ACCS * c + acc + 1)
                if acc < H1_TILES:
                    nc.scalar.activation(h1[:, acc, :], mlp_ps[acc % 2][:, 0:CHUNK], ACT.Relu,
                                         bias=b1_sb[:, acc:acc + 1]).then_inc(h1_taken, 1)
                elif acc < ACCS - 1:
                    m = acc - H1_TILES
                    if m == 0:
                        act.wait_ge(y_out, 16 * (c + 1))
                    nc.scalar.activation(h2[:, m, :], mlp_ps[acc % 2][:, 0:CHUNK], ACT.Relu,
                                         bias=b2_sb[:, m:m + 1]).then_inc(h2_taken, 1)
                else:
                    nc.scalar.copy(y_row, mlp_ps[acc % 2][0:1, 0:CHUNK]).then_inc(y_taken, 1)
                    act.wait_ge(y_taken, c + 2)
                    act.dma_start(out_v[c], y_row.rearrange("o (s j q) -> o s j q", s=MEMBERS,
                                                            j=CHUNK_TILES)).then_inc(y_out, 16)

            def take_tile_acc(tile, acc):
                src = last_ps[tile][acc % 2]
                act.wait_ge(tile_ready[tile], acc + 1)
                if acc < ACCS - 1:
                    bias = b1_sb[:, acc:acc + 1] if acc < H1_TILES else b2_sb[:, acc - H1_TILES:acc - H1_TILES + 1]
                    nc.scalar.activation(last_hidden[tile][:, acc, :], src[:, 0:TILE], ACT.Relu,
                                         bias=bias).then_inc(tile_taken[tile], 1)
                else:
                    nc.scalar.copy(last_y[tile], src[0:1, 0:TILE]).then_inc(tile_taken[tile], 1)
                    act.wait_ge(tile_taken[tile], ACCS)
                    act.dma_start(out_tiles[TILES - CHUNK_TILES + tile], last_y[tile]).then_inc(y_out, 16)

            def emit(kind, which, lap, j):
                if kind == "unit":
                    if which == 0:
                        place_x(lap, j)
                    take_unit(lap, j, which)
                elif kind == "gram":
                    take_batch(*gram_tile(lap, j), which)
                elif kind == "pick" and which + 1 in PICK_END:
                    take_turn(*pick_chunk(lap, j), PICK_END.index(which + 1))
                elif kind == "mlp" and which[1] == LAST_K[which[0]]:
                    take_acc(mlp_chunk(lap, j), which[0])

            for n in range(len(PICKED)):
                act.wait_ge(table_in[n], 16)
                nc.scalar.copy(table_half(0, n), raw_tables[n]).then_inc(high_split, 1)
            for dst, src in ((wp_sb, w_pairs), (wx_sb[:], w_dense_a), (wxb_sb, w_dense_b), (w2_sb[:], w2),
                             (w3_sb[:], w3), (b1_sb[:], b1), (b2_sb[:], b2)):
                act.dma_start(dst, src).then_inc(weights_in, 16)
            steps(emit, 0, range(3))
            act.wait_ge(weights_in, 16 * WEIGHT_DMAS)
            with act.Fori(1, LAPS) as lap:
                steps(emit, lap - 1, [3])
                steps(emit, lap, range(3))
            steps(emit, LAPS - 1, [3])
            for kind, which in tail_events():
                if kind == "gram":
                    take_batch(LAPS - 1, LAP_TILES - 1, which)
                elif which[1] == LAST_K[which[0]] and kind == "mlp":
                    take_acc(CHUNKS - 2, which[0])
                elif which[1] == LAST_K[which[0]]:
                    take_tile_acc(kind[1], which[0])
            act.wait_ge(y_out, 16 * (CHUNKS + 2))

        @block.vector
        def _(dve):
            def build_one_hots(c, picks=range(PICKS)):
                for n in picks:
                    turn, part = PICK_ITEMS[n]
                    of_turn, parts = TURNS[turn]
                    if part == 0:
                        dve.wait_ge(picked_in[turn], 16 * (c + 1))
                    if n >= RING:
                        dve.wait_ge(one_hot_used, PICKS * c + n + 1 - RING)
                    elif not (isinstance(c, int) and c == 0):
                        dve.wait_ge(one_hot_used, PICKS * (c - 1) + max(range(n, PICKS, RING)) + 1)
                    n0 = PICKED.index(of_turn[0])
                    n1 = n0 + len(of_turn)
                    kind = PART_KINDS.index(parts)
                    nc.vector.tensor_scalar(
                        one_hot[:, n % RING, 0:(n1 - n0) * CHUNK],
                        picked_ids_sb[:, n0:n1, :].rearrange("p a m -> p (a m)"),
                        row_sb[:, kind, part:part + 1], None, ALU.is_equal).then_inc(one_hot_ready, 1)

            def split_tables(start, end):
                for n in range(start, end):
                    dve.wait_ge(high_split, n + 1)
                    nc.vector.tensor_tensor(table_half(1, n), raw_tables[n], table_half(0, n).bitcast(F32),
                                            ALU.subtract).then_inc(low_split, 1)

            def split_pairs(c):
                dve.wait_ge(h1_taken, H1_TILES * c + 1)
                for k in range(PAIR_TILES):
                    whole = pairs[:, k].rearrange("r s g -> r (s g)")
                    dve.wait_ge(pairs_in[k], 16 * (c + 1))
                    nc.vector.tensor_copy(pair_halves[:, 0, k, :], whole).then_inc(pairs_high_split, 1)
                    dve.wait_ge(pairs_high_split, PAIR_TILES * c + k + 1)
                    nc.vector.tensor_tensor(pair_halves[:, 1, k, :], whole, pair_halves[:, 0, k, :].bitcast(F32),
                                            ALU.subtract).then_inc(pairs_split, 1)

            dve.wait_ge(row_in, 16)
            build_one_hots(0, range(RING))
            split_tables(0, 2)
            build_one_hots(0, range(RING, PICK_END[0]))
            split_tables(2, 4)
            build_one_hots(0, range(PICK_END[0], PICK_END[1]))
            split_tables(4, len(PICKED))
            build_one_hots(0, range(PICK_END[1], PICKS))
            dve.wait_ge(weights_in, 16 * WEIGHT_DMAS)
            nc.vector.tensor_tensor(wx_sb[:, :], wx_sb[:, :], wxb_sb, ALU.add).then_inc(dense_summed, 1)
            nc.vector.tensor_copy(wp_halves[:, 0], wp_sb).then_inc(wp_split, 1)
            dve.wait_ge(wp_split, 1)
            nc.vector.tensor_tensor(wp_halves[:, 1], wp_sb, wp_halves[:, 0].bitcast(F32),
                                    ALU.subtract).then_inc(wp_split, 1)
            build_one_hots(1)
            with dve.Fori(2, CHUNKS) as c:
                build_one_hots(c)
                split_pairs(c - 2)
            split_pairs(CHUNKS - 2)


def pair_rows():
    feature_at = [0] + [1 + f for f in GATHERED + PICKED]
    index = {}
    for i in range(FEATURES):
        for j in range(i + 1, FEATURES):
            index[i, j] = len(index)
    found = np.zeros((PAIR_ROWS, PAIR_TILES), np.int64)
    for k in range(PAIR_TILES):
        for d in range(SHIFTS):
            for n in range(PAIR_F):
                f = PAIR_F * k + n
                a, b = feature_at[f], feature_at[(f + d + 1) % FEATURES]
                found[d * PAIR_F + n, k] = index[min(a, b), max(a, b)]
    return found


def kernel(**inputs):
    import concourse.bacc as bacc
    from concourse.bass_utils import run_bass_kernel_spmd

    a = {k: np.ascontiguousarray(v) for k, v in inputs.items()}
    w1 = a["W_top1"]
    row_of = np.zeros((PART_ROWS, len(PART_KINDS), max(PART_KINDS)), np.float32)
    for kind, parts in enumerate(PART_KINDS):
        row_of[:, kind, :parts] = np.arange(PART_ROWS * parts).reshape(PART_ROWS, parts)
    arrays = {
        "ids": a["ids"],
        "picked_ids": np.ascontiguousarray(a["ids"][:, PICKED].T),
        "x_t": np.ascontiguousarray(a["r_dense_features"].T),
        "w_pairs": np.ascontiguousarray(w1[DIM:DIM + PAIRS][pair_rows()]),
        "w_dense_a": np.ascontiguousarray(w1[:DIM]),
        "w_dense_b": np.ascontiguousarray(w1[DIM + PAIRS:]),
        "b1": np.ascontiguousarray(a["b_top1"].reshape(H1_TILES, P).T),
        "w2": np.ascontiguousarray(a["W_top2"].reshape(H1_TILES, P, HID2).transpose(1, 0, 2)),
        "b2": np.ascontiguousarray(a["b_top2"].reshape(H2_TILES, P).T),
        "w3": np.ascontiguousarray(a["W_top3"].reshape(H2_TILES, P).T),
        "eye": np.eye(P, dtype=np.float32),
        "row_of": row_of,
    }
    for f in range(TABLES):
        arrays[f"tbl_{f}"] = a[f"tbl_{f}"]
    nc = bacc.Bacc("TRN2", target_bir_lowering=False, num_devices=1)
    ap = {k: nc.dram_tensor(k, v.shape, mybir.dt.from_np(v.dtype), kind="ExternalInput").ap()
          for k, v in arrays.items()}
    out = nc.dram_tensor("y", (BATCH, 1), F32, kind="ExternalOutput").ap()
    build(nc, ap["ids"], ap["picked_ids"], ap["x_t"], [ap[f"tbl_{f}"] for f in range(TABLES)], ap["w_pairs"],
          ap["w_dense_a"], ap["w_dense_b"], ap["b1"], ap["w2"], ap["b2"], ap["w3"], ap["eye"], ap["row_of"], out)
    r = run_bass_kernel_spmd(nc, [arrays], core_ids=[0])
    return r.results[0]["y"]
```
